# Optimizing a Trainium2 kernel written in Bass

```python
import numpy as np
import jax
import jax.numpy as jnp

def _softmax(x, axis=-1):
    return jax.nn.softmax(x, axis=axis)

def _gelu(x):
    return jax.nn.gelu(x, approximate=True)

def _silu(x):
    return jax.nn.silu(x)

def _sigmoid(x):
    return jax.nn.sigmoid(x)

def _layernorm(x, axis=-1, eps=1e-05):
    m = jnp.mean(x, axis=axis, keepdims=True)
    v = jnp.var(x, axis=axis, keepdims=True)
    return (x - m) / jnp.sqrt(v + eps)

def _scatter_add(tgt, idx, src, axis=0):
    return tgt.at[idx].add(src)

def _segment_sum(src, seg, n):
    return jax.ops.segment_sum(src, seg, n)
kernel_name = 'mk_xattn_ffn_d1_seqx_r4_f4103c'

def setup_inputs(seed: int=0):
    np.random.seed(seed)
    _w = jnp.asarray

    def _rec_inputs():
        import jax
        import jax.numpy as jnp
        _rk = jax.random.key(seed)
        x = -7.109e-05 + 0.9999 * jax.random.normal(jax.random.fold_in(_rk, 1), (4, 512, 512), jnp.float32)
        _lenS = 512 - jax.random.randint(jax.random.fold_in(_rk, 7), (4,), 0, max(1, 512 // 4) + 1, jnp.int32)
        _lenS2 = 512 - jax.random.randint(jax.random.fold_in(_rk, 8), (4,), 0, max(1, 512 // 4) + 1, jnp.int32)
        _ctx_512P = jax.random.normal(jax.random.fold_in(_rk, 11), (4, 16, 128), jnp.float32)
        _ctx_512c = jax.random.dirichlet(jax.random.fold_in(_rk, 511), 0.3 * jnp.ones((16,), jnp.float32), (4, 512))
        _ctx_512t = jnp.einsum('bsk,bkd->bsd', _ctx_512c, _ctx_512P)
        _ctx_512t = _ctx_512t * jax.lax.rsqrt(jnp.mean(jnp.square(_ctx_512t)) + 1e-12) * 0.953939
        ctx_512 = 2.81802e-05 + 1.00001 * (_ctx_512t + 0.3 * jax.random.normal(jax.random.fold_in(_rk, 611), (4, 512, 128), jnp.float32))
        return (x, ctx_512)
    x, ctx_512 = _rec_inputs()

    def _L0_xattn_setup():
        import jax, jax.numpy as jnp
        import numpy as np
        EPS = 1e-06
        IMAGE_DIMS = 512
        key = jax.random.key(seed)
        k1, k2, k3 = jax.random.split(key, 3)
        B, I, J, D = (16, 512, 512, 128)
        p = jax.random.normal(k1, (B, I, J), dtype=jnp.float32)
        k_v = jax.random.normal(k2, (B, J, D), dtype=jnp.float32)
        W_k = jax.random.normal(k3, (D, D), dtype=jnp.float32) * (1.0 / np.sqrt(D))
        b_k = jnp.zeros((D,), dtype=jnp.float32)
        ln_gamma = jnp.ones((J,), dtype=jnp.float32)
        ln_beta = jnp.zeros((J,), dtype=jnp.float32)
        return {'p': p, 'k_v': k_v, 'W_k': W_k, 'b_k': b_k, 'ln_gamma': ln_gamma, 'ln_beta': ln_beta}
    _L0_xattn_all = _L0_xattn_setup()
    _L0_xattn_in = {k: v for k, v in _L0_xattn_all.items() if k in ('W_k', 'b_k', 'ln_gamma', 'ln_beta')}
    del _L0_xattn_all

    def _L0_ffn_setup():
        import jax, jax.numpy as jnp
        import numpy as np
        TOP_K = 2
        key = jax.random.key(seed)
        ks = jax.random.split(key, 5)
        B, T, D, E, H = (4, 512, 512, 8, 352)
        s = 1.0 / np.sqrt(D)
        sh = 1.0 / np.sqrt(H)
        return {'x': jax.random.normal(ks[0], (B, T, D), dtype=jnp.float32), 'Wg': jax.random.normal(ks[1], (E, D), dtype=jnp.float32) * s, 'W1': jax.random.normal(ks[2], (E, H, D), dtype=jnp.float32) * s, 'W2': jax.random.normal(ks[3], (E, H, D), dtype=jnp.float32) * s, 'W3': jax.random.normal(ks[4], (E, D, H), dtype=jnp.float32) * sh}
    _L0_ffn_all = _L0_ffn_setup()
    _L0_ffn_in = {k: v for k, v in _L0_ffn_all.items() if k in ('Wg', 'W1', 'W2', 'W3')}
    del _L0_ffn_all
    return {'x': x, 'ctx_512': ctx_512, 'L0_xattn_W_k': _L0_xattn_in['W_k'], 'L0_xattn_b_k': _L0_xattn_in['b_k'], 'L0_xattn_ln_gamma': _L0_xattn_in['ln_gamma'], 'L0_xattn_ln_beta': _L0_xattn_in['ln_beta'], 'L0_ffn_Wg': _L0_ffn_in['Wg'], 'L0_ffn_W1': _L0_ffn_in['W1'], 'L0_ffn_W2': _L0_ffn_in['W2'], 'L0_ffn_W3': _L0_ffn_in['W3']}

def reference(x, ctx_512, L0_xattn_W_k, L0_xattn_b_k, L0_xattn_ln_gamma, L0_xattn_ln_beta, L0_ffn_Wg, L0_ffn_W1, L0_ffn_W2, L0_ffn_W3):
    import jax
    import jax.numpy as jnp

    def _L0_xattn_ref(p, k_v, W_k, b_k, ln_gamma, ln_beta):
        import jax, jax.numpy as jnp
        import numpy as np
        EPS = 1e-06
        IMAGE_DIMS = 512
        kv = k_v @ W_k.T + b_k
        out = jnp.einsum('bij,bjd->bid', p, kv)
        scale = IMAGE_DIMS ** (-0.5)
        sim = jnp.einsum('bid,bjd->bij', out, kv) * scale
        mu = jnp.mean(sim, axis=-1, keepdims=True)
        var = jnp.var(sim, axis=-1, keepdims=True)
        sim = (sim - mu) * jax.lax.rsqrt(var + EPS) * ln_gamma + ln_beta
        attn = jax.nn.softmax(sim, axis=-1)
        return attn

    def _L0_ffn_ref(x, Wg, W1, W2, W3):
        import jax, jax.numpy as jnp
        import numpy as np
        TOP_K = 2
        E = Wg.shape[0]
        scores = jnp.einsum('btd,ed->bte', x, Wg)
        topk_s, topk_i = jax.lax.top_k(scores, TOP_K)
        probs = jax.nn.softmax(topk_s, axis=-1)
        onehot = (topk_i[..., None] == jnp.arange(E)).astype(x.dtype)
        w = jnp.einsum('btk,btke->bte', probs, onehot)
        y = jnp.zeros_like(x)
        for e in range(E):
            h = jax.nn.silu(jnp.einsum('btd,hd->bth', x, W1[e])) * jnp.einsum('btd,hd->bth', x, W2[e])
            y = y + w[..., e:e + 1] * jnp.einsum('bth,dh->btd', h, W3[e])
        return y
    x = x + _L0_xattn_ref(_layernorm(x, axis=-1), ctx_512, L0_xattn_W_k, L0_xattn_b_k, L0_xattn_ln_gamma, L0_xattn_ln_beta)
    x = x + _L0_ffn_ref(_layernorm(x, axis=-1), L0_ffn_Wg, L0_ffn_W1, L0_ffn_W2, L0_ffn_W3)
    return x

_drawn_inputs = setup_inputs


def setup_inputs(seed=0):
    import zlib

    import numpy as np

    out = dict(_drawn_inputs(seed))
    spreads = {'L0_xattn_b_k': (0.0, 2.0),
     'L0_xattn_ln_gamma': (1.0, 0.6),
     'L0_xattn_ln_beta': (0.0, 2.0)}
    factors = {'ctx_512': 2.93, 'L0_xattn_W_k': 5.095}
    for name, (base, spread) in spreads.items():
        noise = np.random.default_rng([zlib.crc32(name.encode()), seed]).standard_normal(out[name].shape)
        drawn = base * np.exp(spread * noise) if base else spread * noise
        out[name] = jnp.asarray(drawn.astype(out[name].dtype))
    for name, factor in factors.items():
        out[name] = (out[name] * factor).astype(out[name].dtype)
    return out
```

```python
from contextlib import ExitStack

import numpy as np
import concourse.bass as bass
from concourse import mybir

ALU = mybir.AluOpType
ACT = mybir.ActivationFunctionType
F32, F16, I32, U32 = mybir.dt.float32, mybir.dt.float16, mybir.dt.int32, mybir.dt.uint32
AX = mybir.AxisListType

P = 128
B, N, D = 4, 512, 512
C = 128
E, H = 8, 352
T = B * N
TPB = N // P
G = T // P
DC = D // P
HCH = [(0, 128), (128, 128), (256, 96)]
HC = len(HCH)
TOPK = 2
NT = (TOPK * T + E * (P - 1)) // P
NQ = NT + 1
ROW = D + 4
XEPS, SEPS = 1e-5, 1e-6
NTHR = T // P


def wait(eng, sem, value):
    if isinstance(value, int) and value <= 0:
        return
    eng.wait_ge(sem, value)


def build(nc, x, xT, ctxT, wkT, bk, gamma, beta, wgT, w12, w3a, w3b, out):
    ctx = ExitStack()
    with ctx:
        def sb(name, shape, dt=F32):
            return ctx.enter_context(nc.sbuf_tensor(name, shape, dt))

        def sem(name):
            return ctx.enter_context(nc.semaphore(name))

        bank = [ctx.enter_context(nc.psum_tensor(f"bank{i}", [P, 512], F32)) for i in range(8)]
        n_table = nc.dram_tensor("n_table", [T, ROW], F32, kind="Internal").ap()

        W12 = sb("W12", [P, E * DC * 2 * H])
        W3 = sb("W3", [P, E * HC * D])
        xT_s = sb("xT_s", [P, DC * N])
        ctx_s = sb("ctx_s", [P, T])
        wk_s = sb("wk_s", [P, C])
        bk_s = sb("bk_s", [P, 1])
        wg_s = sb("wg_s", [P, DC, E])
        gam_s = sb("gam_s", [P, N])
        beta_s = sb("beta_s", [P, N])
        x_s = sb("x_s", [P, TPB, D])
        kv_s = sb("kv_s", [P, N])
        kvg_s = sb("kvg_s", [P, N])
        kvj_s = sb("kvj_s", [P, TPB, C])
        G_s = sb("G_s", [P, C])
        oT_s = sb("oT_s", [P, N])
        prod_s = sb("prod_s", [P, N])
        L_s = sb("L_s", [P, 2, N])
        x1_s = sb("x1_s", [P, 2, D])
        n_s = sb("n_s", [P, 2, D])
        nT_s = sb("nT_s", [P, D])
        junk = sb("junk", [P, D])
        ident = sb("ident", [P, P])
        below = sb("below", [P, P], F16)
        ones16 = sb("ones16", [P, P], F16)
        iota = sb("iota", [P, P])
        thr = sb("thr", [P, NTHR])
        tok1 = sb("tok1", [P, G])
        dump1 = sb("dump1", [P, 1])
        half = sb("half", [P, 1])
        inv_d = sb("inv_d", [P, 1])
        eps_x = sb("eps_x", [P, 1])
        spare_v = sb("spare_v", [1, 1])
        spare_p = sb("spare_p", [1, 1])
        ones = sb("ones", [P, 1])
        zero8 = sb("zero8", [P, E])
        ksum = sb("ksum", [P, 1])
        kneg = sb("kneg", [P, 1])
        msq = sb("msq", [P, TPB])
        bn = sb("bn", [P, 2, 6])
        mv = sb("mv", [P, 2, 2])
        va = sb("va", [P, 2])
        alpha = sb("alpha", [P, 2])
        lmin = sb("lmin", [P, 2])
        esum = sb("esum", [P, 2])
        einv = sb("einv", [P, 2])
        xsum = sb("xsum", [P, 2])
        xneg = sb("xneg", [P, 2])
        ssq = sb("ssq", [P, 2])
        vd = sb("vd", [P, 2])
        vr = sb("vr", [P, 2])
        rstd = sb("rstd", [P, 2])
        sc = sb("sc", [P, E])
        top = sb("top", [P, TPB, 8])
        topi = sb("topi", [P, TPB, 8], U32)
        dlt = sb("dlt", [P, G])
        edl = sb("edl", [P, G])
        wden = sb("wden", [P, G])
        wrow = sb("wrow", [P, G, 4])
        oh = sb("oh", [P, G, TOPK, E], F16)
        cnt = sb("cnt", [P, E])
        cmp_n = sb("cmp_n", [P, E, NTHR])
        ntile = sb("ntile", [P, E])
        tend = sb("tend", [P, E])
        start = sb("start", [P, E])
        base = sb("base", [P, G, E])
        pick = sb("pick", [P, G * TOPK, E])
        pos = sb("pos", [P, G * TOPK])
        posi = sb("posi", [P, G * TOPK], I32)
        qi = sb("qi", [P, G * TOPK], I32)
        ri = sb("ri", [P, G * TOPK], I32)
        qf = sb("qf", [P, G * TOPK])
        rf = sb("rf", [P, G * TOPK])
        tfree = sb("tfree", [P, 2 * NQ])
        gidx = sb("gidx", [P, NQ], U32)
        sidx = sb("sidx", [P, NQ], U32)
        gcol = sb("gcol", [P, 2], U32)
        scol = sb("scol", [P, 2], U32)
        ecol = sb("ecol", [P, NQ])
        ecoli = sb("ecoli", [P, NQ], I32)
        oh_r = xT_s[:, 0:G * TOPK * P // 2].bitcast(F16).rearrange("p (c r) -> p c r", r=P)
        oh_q = ctx_s[:, 0:G * TOPK * NQ // 2].bitcast(F16).rearrange("p (c q) -> p c q", q=NQ)
        cmp_t = ctx_s[:, 1024:1024 + NQ * E].rearrange("p (t e) -> p t e", e=E)
        zrow = prod_s
        x_flat = x_s[:, :, :].rearrange("p a n -> p (a n)")
        ng = [x_flat[:, k * ROW:(k + 1) * ROW] for k in range(2)]
        nTm = [kvg_s[:, :], kv_s[:, :]]
        act_a = [L_s[:, k, 0:H] for k in range(2)]
        hid = [x1_s[:, k, 0:H] for k in range(2)]
        hT = [n_s[:, k, 0:HC * P].rearrange("p (c m) -> p c m", m=P) for k in range(2)]
        ym = [oT_s[:, :], kvj_s[:, :, :].rearrange("p a n -> p (a n)")]
        wm = sb("wm", [P, 2])
        wsel = sb("wsel", [P, 2])
        wmul = sb("wmul", [P, 2])

        s_const = sem("s_const")
        s_cin = sem("s_cin")
        s_xT = sem("s_xT")
        s_xl = [sem(f"s_xl{i}") for i in range(TPB)]
        s_wt = sem("s_wt")
        s_stx = [sem(f"s_stx{i}") for i in range(2)]
        s_stn = [sem(f"s_stn{i}") for i in range(2)]
        s_wst = sem("s_wst")
        s_zr = sem("s_zr")
        s_ngam = sem("s_ngam")
        s_kvp, s_kv, s_kneg, s_kvc, s_kvjp, s_kvj = [sem(n) for n in ("s_kvp", "s_kv", "s_kneg", "s_kvc", "s_kvjp", "s_kvj")]
        s_Gp, s_G, s_op, s_o, s_ogp, s_prod, s_mp, s_msq, s_kvg = [
            sem(n) for n in ("s_Gp", "s_G", "s_op", "s_o", "s_ogp", "s_prod", "s_mp", "s_msq", "s_kvg")]
        s_dl, s_ed, s_wd, s_w1, s_w2, s_wi = [sem(n) for n in ("s_dl", "s_ed", "s_wd", "s_w1", "s_w2", "s_wi")]
        s_bn, s_mv, s_va, s_al, s_S, s_T, s_L, s_E, s_ei, s_x1 = [
            sem(n) for n in ("s_bn", "s_mv", "s_va", "s_al", "s_S", "s_T", "s_L", "s_E", "s_ei", "s_x1")]
        s_xn, s_sq, s_vd, s_vr, s_rs, s_n, s_nTp, s_nT, s_scp, s_sc, s_top, s_ti = [
            sem(n) for n in ("s_xn", "s_sq", "s_vd", "s_vr", "s_rs", "s_n", "s_nTp", "s_nT", "s_scp", "s_sc", "s_top", "s_ti")]
        s_r = sem("s_r")
        s_oh, s_cntp, s_ohq, s_rq, s_ohr, s_tab, s_et = [
            sem(n) for n in ("s_oh", "s_cntp", "s_ohq", "s_rq", "s_ohr", "s_tab", "s_et")]
        s_idx = sem("s_idx")
        s_ng = [sem(f"s_ng{i}") for i in range(2)]
        s_mTp, s_mT, s_ap, s_a, s_bp, s_h, s_hTp, s_hT, s_yp, s_y, s_ws, s_wm = [
            sem(n) for n in ("s_mTp", "s_mT", "s_ap", "s_a", "s_bp", "s_h", "s_hTp", "s_hT", "s_yp", "s_y", "s_ws", "s_wm")]
        s_sct, s_gc, s_scc = sem("s_sct"), sem("s_gc"), sem("s_scc")

        NCONST = 14

        def hold(eng, *waits):
            for s, v in waits:
                wait(eng, s, v)
            if all(isinstance(v, int) for _, v in waits):
                return
            if eng is nc.vector or eng.engine == nc.vector.engine:
                eng.memset(spare_v[:, :], 0.0)
            else:
                eng.tensor_tensor(spare_p[0:1, 0:1], half[0:1, :], half[0:1, :], ALU.add)

        def lag(b, i, k):
            while k > i:
                b, i = b - 1, i + TPB
            return b, i - k

        def real(b):
            return not isinstance(b, int) or 0 <= b < B

        def batches(eng, body):
            body(0)
            with eng.Fori(1, B - 1) as b:
                body(b)
            body(B - 1)
            body(B)

        def g_of(b, i):
            return b * TPB + i

        FIRST, PAIRS = 3, (NT - 2 - 3) // 2

        def expert_tiles(eng, body):
            for t in range(FIRST):
                body(t // 2, t % 2)
            with eng.Fori(FIRST // 2, FIRST // 2 + PAIRS) as j:
                body(j, 1)
                body(j + 1, 0)
            for t in range(FIRST + 2 * PAIRS, NT + 1):
                body(t // 2, t % 2)

        def exists(t):
            return not isinstance(t, int) or 0 <= t < NT

        block = ctx.enter_context(nc.Block())

        @block.sync
        def _(eng):
            xrows = x.rearrange("(g p) d -> g p d", p=P)
            orows = out[0:T, :].rearrange("(g p) d -> g p d", p=P)
            nrows = n_table.rearrange("(g p) d -> g p d", p=P)
            for dst, src in ((wk_s[:, :], wkT), (ctx_s[:, 0:N], ctxT[:, 0:N]), (bk_s[:, :], bk)):
                eng.dma_start(dst, src).then_inc(s_cin, 16)
            eng.dma_start(xT_s[:, :], xT[0]).then_inc(s_xT, 16)
            for dst, src in ((gam_s[:, :], gamma.to_broadcast([P, N])), (beta_s[:, :], beta.to_broadcast([P, N])),
                             (wg_s[:, :, :], wgT), (ctx_s[:, N:T], ctxT[:, N:T])):
                eng.dma_start(dst, src).then_inc(s_cin, 16)
            for i in range(TPB):
                eng.dma_start(x_s[:, i, :], xrows[i]).then_inc(s_xl[i], 16)

            def body(b):
                ahead = not isinstance(b, int) or b < B - 1
                if real(b) and ahead:
                    eng.wait_ge(s_op, b + 1)
                    eng.dma_start(xT_s[:, :], xT[bass.ds(b + 1, 1)].rearrange("a p n -> p (a n)")).then_inc(s_xT, 16)
                for i in range(TPB):
                    if real(b):
                        g = g_of(b, i)
                        eng.wait_ge(s_x1, g + 1)
                        eng.dma_start(orows[bass.ds(g, 1)].rearrange("a p d -> (a p) d"), x1_s[:, i % 2, :]).then_inc(s_stx[i % 2], 16)
                        if ahead:
                            eng.dma_start(x_s[:, i, :], xrows[bass.ds(g + TPB, 1)].rearrange("a p d -> (a p) d")).then_inc(s_xl[i], 16)
                        eng.wait_ge(s_n, g + 1)
                        eng.dma_start(nrows[bass.ds(g, 1), :, 0:D].rearrange("a p d -> (a p) d"), n_s[:, i % 2, :]).then_inc(s_stn[i % 2], 16)
                if isinstance(b, int) and b == 0:
                    return
                eng.wait_ge(s_w2, b)
                eng.wait_ge(s_wi, b)
                eng.dma_start(nrows[bass.ds((b - 1) * TPB, TPB), :, D:ROW].rearrange("g p k -> p g k"),
                              wrow[:, bass.ds((b - 1) * TPB, TPB), :]).then_inc(s_wst, 16)
            batches(eng, body)
            eng.wait_ge(s_zr, 1)
            eng.dma_start(out[T:T + P, :], zrow[:, :]).then_inc(s_cin, 16)
            eng.wait_ge(s_sct, 16 * NT)

        @block.gpsimd
        def _(eng):
            eng.memset(ident[:, :], 0.0).then_inc(s_const, 1)
            eng.memset(below[:, :], 1.0).then_inc(s_const, 1)
            eng.memset(ones[:, :], 1.0).then_inc(s_const, 1)
            eng.memset(half[:, :], -0.5).then_inc(s_const, 1)
            eng.memset(inv_d[:, :], 1.0 / D).then_inc(s_const, 1)
            eng.memset(eps_x[:, :], XEPS).then_inc(s_const, 1)
            eng.wait_ge(s_const, 6)
            eng.affine_select(out=ident[:, :], in_=ident[:, :], compare_op=ALU.not_equal, fill=1.0, base=0,
                              pattern=[[-1, P]], channel_multiplier=1).then_inc(s_const, 1)
            eng.affine_select(out=below[:, :], in_=below[:, :], compare_op=ALU.is_gt, fill=0.0, base=0,
                              pattern=[[1, P]], channel_multiplier=-1).then_inc(s_const, 1)
            eng.memset(ones16[:, :], 1.0).then_inc(s_const, 1)
            eng.memset(zero8[:, :], 0.0).then_inc(s_const, 1)
            for dst, step, n, first, mul in ((iota, 1, P, 0, 0), (thr, P, NTHR, 0, 0), (tok1, P, G, 1, 1), (dump1, 0, 1, T + 1, 1)):
                eng.iota(dst[:, :], [[step, n]], base=first, channel_multiplier=mul,
                         allow_small_or_imprecise_dtypes=True).then_inc(s_const, 1)

            def body(b):
                for i in range(TPB):
                    if real(b):
                        g, k = g_of(b, i), i % 2
                        eng.wait_ge(s_va, g + 1)
                        wait(eng, s_T, g - 1)
                        eng.tensor_tensor(alpha[:, k:k + 1], va[:, k:k + 1], half[:, :], ALU.pow).then_inc(s_al, 1)
                    b2, i2 = lag(b, i, 2)
                    if real(b2):
                        g, k = g_of(b2, i2), i2 % 2
                        eng.wait_ge(s_sq, g + 1)
                        eng.tensor_tensor(vd[:, k:k + 1], ssq[:, k:k + 1], inv_d[:, :], ALU.mult).then_inc(s_vd, 1)
                        eng.wait_ge(s_vd, g + 1)
                        eng.tensor_tensor(vr[:, k:k + 1], vd[:, k:k + 1], eps_x[:, :], ALU.add).then_inc(s_vr, 1)
                        eng.wait_ge(s_vr, g + 1)
                        wait(eng, s_n, g - 1)
                        eng.tensor_tensor(rstd[:, k:k + 1], vr[:, k:k + 1], half[:, :], ALU.pow).then_inc(s_rs, 1)
            batches(eng, body)

            eng.wait_ge(s_ohq, 1)
            eng.wait_ge(s_const, NCONST)
            eng.tensor_tensor(oh_q.rearrange("p (g k) q -> p g (k q)", k=TOPK), oh_q.rearrange("p (g k) q -> p g (k q)", k=TOPK),
                              tok1[:, :, None].to_broadcast([P, G, TOPK * NQ]), ALU.mult).then_inc(s_rq, 1)

            eng.wait_ge(s_idx, 2)
            for i in range(2):
                eng.wait_ge(s_stx[i], 16 * G // 2)
                eng.wait_ge(s_stn[i], 16 * G // 2)
            eng.wait_ge(s_wst, 16 * B)
            eng.wait_ge(s_cin, 16 * 8)

            def gather(j, r):
                t = 2 * j + r
                if not exists(t):
                    return
                wait(eng, s_mTp, t - 1)
                wait(eng, s_ws, t - 1)
                wait(eng, s_wm, t - 1)
                eng.tensor_copy(gcol[:, r:r + 1], gidx[:, bass.ds(t, 1)]).then_inc(s_gc, 1)
                hold(eng, (s_gc, t + 1))
                eng.indirect_dma_start(out=ng[r], out_offset=None, in_=n_table,
                                       in_offset=bass.IndirectOffsetOnAxis(ap=gcol[:, r:r + 1], axis=0)).then_inc(s_ng[r], 16)

            def body(j, r):
                gather(j + 1, r)
                t = 2 * j + r - 1
                if exists(t):
                    eng.tensor_copy(scol[:, 1 - r:2 - r], sidx[:, bass.ds(t, 1)]).then_inc(s_scc, 1)
                    hold(eng, (s_scc, t + 1), (s_y, t + 1), (s_sct, 16 * t))
                    eng.indirect_dma_start(out=out, out_offset=bass.IndirectOffsetOnAxis(ap=scol[:, 1 - r:2 - r], axis=0),
                                           in_=ym[1 - r], in_offset=None, compute_op=ALU.add).then_inc(s_sct, 16)
            gather(0, 0)
            gather(0, 1)
            expert_tiles(eng, body)

        @block.scalar
        def _(eng):
            eng.wait_ge(s_xl[0], 16)
            w3v = W3[:, :].rearrange("p (e c d) -> p e c d", e=E, c=HC)
            for e in range(E):
                n = DC * 2 * H
                eng.dma_start(W12[:, e * n:(e + 1) * n], w12[e]).then_inc(s_wt, 16)
                eng.dma_start(w3v[:, e, 0:2, :], w3a[e]).then_inc(s_wt, 16)
                eng.dma_start(w3v[0:HCH[2][1], e, 2, :], w3b[e]).then_inc(s_wt, 16)

            def kv_evac(b):
                eng.wait_ge(s_kvp, b + 1)
                wait(eng, s_kvg, b)
                wait(eng, s_kneg, b)
                eng.activation(kv_s[:, :], bank[0][:, :], ACT.Identity, bias=bk_s[:, 0:1], accum_out=ksum[:, 0:1]).then_inc(s_kv, 1)

            def kvj_evac(b):
                eng.wait_ge(s_kvjp, b + 1)
                wait(eng, s_op, b)
                eng.activation(kvj_s[:, :, :].rearrange("p a n -> p (a n)"), bank[1][:, :], ACT.Copy).then_inc(s_kvj, 1)

            def o_evac(b):
                eng.wait_ge(s_op, b + 1)
                wait(eng, s_S, TPB * b)
                wait(eng, s_prod, b)
                eng.activation(oT_s[:, :], bank[1][:, :], ACT.Copy).then_inc(s_o, 1)

            def body(b):
                ahead = not isinstance(b, int) or b < B - 1
                for i in range(TPB):
                    b2, i2 = lag(b, i, 2)
                    if real(b2):
                        g, k = g_of(b2, i2), i2 % 2
                        eng.wait_ge(s_xn, g + 1)
                        wait(eng, s_vd, g - 1)
                        eng.activation(junk[:, :], x1_s[:, k, :], ACT.Square, bias=xneg[:, k:k + 1],
                                       accum_out=ssq[:, k:k + 1]).then_inc(s_sq, 1)
                    if real(b):
                        g, k = g_of(b, i), i % 2
                        eng.wait_ge(s_S, g + 1)
                        eng.wait_ge(s_al, g + 1)
                        wait(eng, s_x1, g - 1)
                        eng.activation(L_s[:, k, :], bank[2 + i][:, :], ACT.Copy, scale=alpha[:, k:k + 1]).then_inc(s_T, 1)
                    b1, i1 = lag(b, i, 1)
                    if real(b1):
                        g, k = g_of(b1, i1), i1 % 2
                        eng.wait_ge(s_L, g + 1)
                        wait(eng, s_ei, g - 1)
                        eng.activation(L_s[:, k, :], L_s[:, k, :], ACT.Exp, scale=-1.0, bias=lmin[:, k:k + 1],
                                       accum_out=esum[:, k:k + 1]).then_inc(s_E, 1)
                    b3, i3 = lag(b, i, 3)
                    if real(b3):
                        g = g_of(b3, i3)
                        eng.wait_ge(s_nTp, g + 1)
                        wait(eng, s_scp, g)
                        eng.activation(nT_s[:, :], bank[6][:, :], ACT.Copy).then_inc(s_nT, 1)
                    if real(b) and ahead:
                        if i == 0:
                            kv_evac(b + 1)
                        if i == 1:
                            kvj_evac(b + 1)
                        if i == 3:
                            o_evac(b + 1)
                if isinstance(b, int) and b == 0:
                    return
                eng.wait_ge(s_dl, b)
                eng.activation(edl[:, bass.ds((b - 1) * TPB, TPB)], dlt[:, bass.ds((b - 1) * TPB, TPB)], ACT.Exp).then_inc(s_ed, 1)

            eng.wait_ge(s_cin, 16 * 7)
            kv_evac(0)
            kvj_evac(0)
            o_evac(0)
            batches(eng, body)

            def mT_evac(j, r):
                t = 2 * j + r
                if exists(t):
                    eng.wait_ge(s_mTp, t + 1)
                    wait(eng, s_bp, t - 1)
                    eng.activation(nTm[r], bank[5][:, :], ACT.Copy).then_inc(s_mT, 1)

            def tile(j, r):
                t = 2 * j + r
                if exists(t):
                    eng.wait_ge(s_ap, t + 1)
                    wait(eng, s_h, t - 1)
                    eng.activation(act_a[r], bank[r][:, 0:H], ACT.Silu).then_inc(s_a, 1)
                if exists(t - 1):
                    eng.wait_ge(s_hTp, t)
                    wait(eng, s_yp, t - 2)
                    for c, (_, n) in enumerate(HCH):
                        if c == 0:
                            eng.activation(hT[1 - r][:, 0:2, :].rearrange("p c m -> p (c m)"), bank[6][:, 0:2 * P], ACT.Copy).then_inc(s_hT, 1)
                        if c == 2:
                            eng.activation(hT[1 - r][0:n, 2, :], bank[6][0:n, 2 * P:3 * P], ACT.Copy).then_inc(s_hT, 1)
                mT_evac(j + (1 if r else 0), 1 - r)
                if exists(t - 1):
                    eng.wait_ge(s_yp, t)
                    eng.wait_ge(s_wm, t)
                    wait(eng, s_sct, 16 * (t - 2))
                    eng.activation(ym[1 - r], bank[4 if r else 7][:, :], ACT.Copy, scale=wm[:, 1 - r:2 - r]).then_inc(s_y, 1)
            mT_evac(0, 0)
            expert_tiles(eng, tile)

        @block.vector
        def _(eng):
            eng.wait_ge(s_cin, 16 * 7)
            eng.tensor_scalar(gam_s[:, :], gam_s[:, :], -1.0, None, ALU.mult).then_inc(s_ngam, 1)
            eng.tensor_scalar(beta_s[:, :], beta_s[:, :], -1.0, None, ALU.mult).then_inc(s_ngam, 1)

            def centre_keys(b):
                eng.wait_ge(s_kv, b + 1)
                eng.tensor_scalar(kneg[:, :], ksum[:, :], -1.0 / N, None, ALU.mult).then_inc(s_kneg, 1)
                eng.wait_ge(s_kneg, b + 1)
                eng.tensor_scalar(kv_s[:, :], kv_s[:, :], kneg[:, 0:1], None, ALU.add).then_inc(s_kvc, 1)

            def gram_copy(b):
                eng.wait_ge(s_Gp, b + 1)
                wait(eng, s_ogp, b)
                eng.tensor_scalar(G_s[:, :], bank[0][:, 0:C], 1.0 / N, None, ALU.mult).then_inc(s_G, 1)

            def gamma_keys(b):
                eng.wait_ge(s_kvc, b + 1)
                eng.wait_ge(s_ngam, 2)
                wait(eng, s_S, TPB * b)
                eng.tensor_tensor(kvg_s[:, :], kv_s[:, :], gam_s[:, :], ALU.mult).then_inc(s_kvg, 1)

            def mean_square(b):
                eng.wait_ge(s_ogp, b + 1)
                eng.wait_ge(s_o, b + 1)
                wait(eng, s_mp, b)
                eng.tensor_tensor(prod_s[:, :], bank[0][:, :], oT_s[:, :], ALU.mult).then_inc(s_prod, 1)
                eng.wait_ge(s_mp, b + 1)
                eng.tensor_scalar(msq[:, :], bank[1][:, 0:TPB], N * SEPS * XEPS, None, ALU.add).then_inc(s_msq, 1)

            def x_stats(b, i):
                g, k = g_of(b, i), i % 2
                eng.wait_ge(s_xl[i], 16 * (b + 1))
                eng.bn_stats(bn[:, k, :], x_s[:, i, :]).then_inc(s_bn, 1)
                hold(eng, (s_bn, g + 1))
                eng.bn_aggr(mv[:, k, :], bn[:, k, :]).then_inc(s_mv, 1)

            def body(b):
                ahead = not isinstance(b, int) or b < B - 1
                for i in range(TPB):
                    bn_, in_ = (b, i + 1) if i + 1 < TPB else (b + 1, 0)
                    if real(b) and (ahead or i + 1 < TPB):
                        x_stats(bn_, in_)
                    if real(b):
                        g, k = g_of(b, i), i % 2
                        eng.wait_ge(s_mv, g + 1)
                        eng.wait_ge(s_msq, b + 1)
                        wait(eng, s_al, g - 1)
                        eng.tensor_scalar(va[:, k:k + 1], mv[:, k, 1:2], N * SEPS, msq[:, i:i + 1], ALU.mult, ALU.add).then_inc(s_va, 1)
                        hold(eng, (s_T, g + 1), (s_E, g - 1))
                        eng.tensor_tensor_reduce(L_s[:, k, :], L_s[:, k, :], beta_s[:, :], 1.0, 3.0e38, ALU.add, ALU.min,
                                                 lmin[:, k:k + 1]).then_inc(s_L, 1)
                    b1, i1 = lag(b, i, 1)
                    if real(b1):
                        g, k = g_of(b1, i1), i1 % 2
                        eng.wait_ge(s_E, g + 1)
                        eng.reciprocal(einv[:, k:k + 1], esum[:, k:k + 1]).then_inc(s_ei, 1)
                        eng.wait_ge(s_ei, g + 1)
                        wait(eng, s_stx[k], 16 * (b1 * TPB // 2 + i1 // 2))
                        wait(eng, s_sq, g - 1)
                        eng.scalar_tensor_tensor(x1_s[:, k, :], L_s[:, k, :], einv[:, k:k + 1], x_s[:, i1, :], ALU.mult, ALU.add,
                                                 accum_out=xsum[:, k:k + 1]).then_inc(s_x1, 1)
                        eng.wait_ge(s_x1, g + 1)
                        eng.tensor_scalar(xneg[:, k:k + 1], xsum[:, k:k + 1], -1.0 / D, None, ALU.mult).then_inc(s_xn, 1)
                    b2, i2 = lag(b, i, 2)
                    if real(b2):
                        g, k = g_of(b2, i2), i2 % 2
                        eng.wait_ge(s_rs, g + 1)
                        eng.wait_ge(s_xn, g + 1)
                        wait(eng, s_stn[k], 16 * (b2 * TPB // 2 + i2 // 2))
                        wait(eng, s_nTp, g - 1)
                        eng.tensor_scalar(n_s[:, k, :], x1_s[:, k, :], xneg[:, k:k + 1], rstd[:, k:k + 1], ALU.add, ALU.mult).then_inc(s_n, 1)
                    b4, i4 = lag(b, i, 4)
                    if real(b4):
                        g = g_of(b4, i4)
                        eng.wait_ge(s_scp, g + 1)
                        wait(eng, s_ti, g)
                        eng.tensor_copy(sc[:, :], bank[7][:, 0:E]).then_inc(s_sc, 1)
                        hold(eng, (s_sc, g + 1))
                        eng.max(top[:, i4, :], sc[:, :]).then_inc(s_top, 1)
                        hold(eng, (s_top, g + 1))
                        eng.max_index(topi[:, i4, :], top[:, i4, :], sc[:, :]).then_inc(s_ti, 1)
                    if real(b) and ahead:
                        if i == 0:
                            centre_keys(b + 1)
                        if i == 2:
                            gram_copy(b + 1)
                        if i == 3:
                            gamma_keys(b + 1)
                            mean_square(b + 1)
                if isinstance(b, int) and b == 0:
                    return
                cols = bass.ds((b - 1) * TPB, TPB)
                eng.wait_ge(s_ti, TPB * b)
                eng.tensor_tensor(dlt[:, cols], top[:, :, 1],
                                  top[:, :, 0], ALU.subtract).then_inc(s_dl, 1)
                eng.tensor_copy(wrow[:, cols, 2:4], topi[:, :, 0:2]).then_inc(s_wi, 1)
                eng.wait_ge(s_ed, b)
                eng.tensor_scalar(wden[:, cols], edl[:, cols], 1.0, None, ALU.add).then_inc(s_wd, 1)
                eng.wait_ge(s_wd, b)
                w1 = wrow[:, cols, 0:1].rearrange("p g a -> p (g a)")
                w2 = wrow[:, cols, 1:2].rearrange("p g a -> p (g a)")
                eng.reciprocal(w1, wden[:, cols]).then_inc(s_w1, 1)
                eng.wait_ge(s_w1, b)
                eng.tensor_tensor(w2, edl[:, cols], w1, ALU.mult).then_inc(s_w2, 1)

            x_stats(0, 0)
            centre_keys(0)
            gram_copy(0)
            gamma_keys(0)
            mean_square(0)
            batches(eng, body)

            steps = [0]

            def then(ins):
                steps[0] += 1
                ins.then_inc(s_r, 1)
                eng.wait_ge(s_r, steps[0])

            eng.wait_ge(s_mp, B)
            eng.memset(zrow[:, :], 0.0).then_inc(s_zr, 1)
            eng.wait_ge(s_const, NCONST)
            eng.wait_ge(s_wi, B)
            eng.tensor_tensor(oh[:, :, :, :], wrow[:, :, 2:4, None].to_broadcast([P, G, TOPK, E]),
                              iota[:, None, None, 0:E].to_broadcast([P, G, TOPK, E]), ALU.is_equal).then_inc(s_oh, 1)
            eng.wait_ge(s_cntp, 1)
            then(eng.tensor_reduce(cnt[:, :], bank[1][:, 0:G * TOPK * E].rearrange("p (c e) -> p e c", e=E), AX.X, ALU.add))
            then(eng.tensor_tensor(cmp_n[:, :, :], cnt[:, :, None].to_broadcast([P, E, NTHR]),
                                   thr[:, None, :].to_broadcast([P, E, NTHR]), ALU.is_gt))
            then(eng.tensor_reduce(ntile[:, :], cmp_n[:, :, :], AX.X, ALU.add))
            then(eng.tensor_tensor_scan(tend[:, :], ntile[:, :], zero8[:, :], 0.0, ALU.add, ALU.add))
            then(eng.tensor_tensor(start[:, :], tend[:, :], ntile[:, :], ALU.subtract))
            then(eng.tensor_scalar(start[:, :], start[:, :], float(P), None, ALU.mult))
            then(eng.tensor_tensor(base[:, :, :], bank[0][:, 0:G * E].rearrange("p (g e) -> p g e", e=E),
                                   start[:, None, :].to_broadcast([P, G, E]), ALU.add))
            then(eng.tensor_tensor(pick[:, :, :].rearrange("p (g k) e -> p g k e", k=TOPK), oh[:, :, :, :],
                                   base[:, :, None, :].to_broadcast([P, G, TOPK, E]), ALU.mult))
            then(eng.tensor_reduce(pos[:, :], pick[:, :, :], AX.X, ALU.add))
            then(eng.tensor_copy(posi[:, :], pos[:, :]))
            eng.tensor_scalar(ri[:, :], posi[:, :], P - 1, None, ALU.bitwise_and).then_inc(s_r, 1)
            eng.tensor_scalar(qi[:, :], posi[:, :], 7, None, ALU.arith_shift_right).then_inc(s_r, 1)
            steps[0] += 2
            eng.wait_ge(s_r, steps[0])
            eng.tensor_copy(qf[:, :], qi[:, :]).then_inc(s_r, 1)
            steps[0] += 1
            then(eng.tensor_copy(rf[:, :], ri[:, :]))
            eng.tensor_tensor(oh_q, qf[:, :, None].to_broadcast([P, G * TOPK, NQ]),
                              iota[:, None, 0:NQ].to_broadcast([P, G * TOPK, NQ]), ALU.is_equal).then_inc(s_ohq, 1)
            eng.tensor_tensor(oh_r, rf[:, :, None].to_broadcast([P, G * TOPK, P]),
                              iota[:, None, :].to_broadcast([P, G * TOPK, P]), ALU.is_equal).then_inc(s_ohr, 1)
            then(eng.tensor_tensor(cmp_t, iota[:, 0:NQ, None].to_broadcast([P, NQ, E]),
                                   tend[:, None, :].to_broadcast([P, NQ, E]), ALU.is_ge))
            then(eng.tensor_reduce(ecol[:, :], cmp_t, AX.X, ALU.add))
            then(eng.tensor_scalar(ecol[:, :], ecol[:, :], float(E - 1), None, ALU.min))
            eng.tensor_copy(ecoli[:, :], ecol[:, :]).then_inc(s_et, 1)
            eng.wait_ge(s_tab, 1)
            eng.tensor_scalar(gidx[:, :], bank[2][:, 0:NQ], -1.0, 0.0, ALU.add, ALU.max).then_inc(s_idx, 1)
            then(eng.tensor_scalar(tfree[:, 0:NQ], bank[2][:, 0:NQ], 0.0, dump1[:, 0:1], ALU.is_equal, ALU.mult))
            eng.scalar_tensor_tensor(sidx[:, :], bank[2][:, 0:NQ], -1.0, tfree[:, 0:NQ], ALU.add, ALU.add).then_inc(s_idx, 1)

            def tile(j, r):
                t = 2 * j + r
                if not exists(t):
                    return
                eng.wait_ge(s_ng[r], 16 * (j + 1))
                wait(eng, s_wm, t)
                eng.tensor_scalar(wsel[:, :], ng[r][:, D + 2:D + 4], ecol[:, bass.ds(t, 1)], None, ALU.is_equal).then_inc(s_ws, 1)
                hold(eng, (s_ws, t + 1), (s_y, t - 1))
                eng.tensor_tensor_reduce(wmul[:, :], wsel[:, :], ng[r][:, D:D + 2], 1.0, 0.0, ALU.mult, ALU.add,
                                         wm[:, r:r + 1]).then_inc(s_wm, 1)
                eng.wait_ge(s_a, t + 1)
                eng.wait_ge(s_bp, t + 1)
                wait(eng, s_hTp, t - 1)
                eng.tensor_tensor(hid[r], act_a[r], bank[2 + r][:, 0:H], ALU.mult).then_inc(s_h, 1)
            expert_tiles(eng, tile)

        @block.tensor
        def _(eng):
            def keys(b):
                wait(eng, s_prod, b)
                eng.matmul(bank[0][:, :], wk_s[:, :], ctx_s[:, bass.ds(b * N, N)], start=True, stop=True).then_inc(s_kvp, 1)

            def turn_keys(b):
                eng.wait_ge(s_kvc, b + 1)
                wait(eng, s_msq, b)
                for c in range(TPB):
                    mm = eng.transpose(bank[1][:, c * C:(c + 1) * C], kv_s[:, c * P:(c + 1) * P], ident[:, :])
                mm.then_inc(s_kvjp, 1)

            def gram(b):
                eng.wait_ge(s_kvj, b + 1)
                eng.wait_ge(s_kv, b + 1)
                for c in range(TPB):
                    mm = eng.matmul(bank[0][:, 0:C], kvj_s[:, c, :], kvj_s[:, c, :], start=(c == 0), stop=(c == TPB - 1))
                mm.then_inc(s_Gp, 1)

            def outs(b):
                eng.wait_ge(s_xT, 16 * (b + 1))
                eng.wait_ge(s_kvj, b + 1)
                for c in range(DC):
                    mm = eng.matmul(bank[1][:, :], kvj_s[:, c, :], xT_s[:, c * N:(c + 1) * N], start=(c == 0), stop=(c == DC - 1))
                mm.then_inc(s_op, 1)

            def squares(b):
                eng.wait_ge(s_G, b + 1)
                eng.wait_ge(s_o, b + 1)
                eng.matmul(bank[0][:, :], G_s[:, :], oT_s[:, :], start=True, stop=True).then_inc(s_ogp, 1)
                eng.wait_ge(s_prod, b + 1)
                for i in range(TPB):
                    mm = eng.matmul(bank[1][:, i:i + 1], prod_s[:, i * P:(i + 1) * P], ones[:, 0:1], start=True, stop=True)
                mm.then_inc(s_mp, 1)

            def body(b):
                ahead = not isinstance(b, int) or b < B - 1
                for i in range(TPB):
                    if real(b):
                        g = g_of(b, i)
                        eng.wait_ge(s_o, b + 1)
                        eng.wait_ge(s_kvg, b + 1)
                        wait(eng, s_T, g - TPB + 1)
                        eng.matmul(bank[2 + i][:, :], oT_s[:, i * P:(i + 1) * P], kvg_s[:, :], start=True, stop=True).then_inc(s_S, 1)
                    b3, i3 = lag(b, i, 3)
                    if real(b3):
                        g, k = g_of(b3, i3), i3 % 2
                        eng.wait_ge(s_n, g + 1)
                        wait(eng, s_nT, g)
                        for c in range(DC):
                            mm = eng.transpose(bank[6][:, c * P:(c + 1) * P], n_s[:, k, c * P:(c + 1) * P], ident[:, :])
                        mm.then_inc(s_nTp, 1)
                    b4, i4 = lag(b, i, 4)
                    if real(b4):
                        g = g_of(b4, i4)
                        eng.wait_ge(s_nT, g + 1)
                        wait(eng, s_sc, g)
                        for c in range(DC):
                            mm = eng.matmul(bank[7][:, 0:E], nT_s[:, c * P:(c + 1) * P], wg_s[:, c, :], start=(c == 0), stop=(c == DC - 1))
                        mm.then_inc(s_scp, 1)
                    if real(b) and ahead:
                        if i == 0:
                            keys(b + 1)
                        if i == 1:
                            turn_keys(b + 1)
                        if i == 2:
                            gram(b + 1)
                        if i == 3:
                            outs(b + 1)
                            squares(b + 1)

            eng.wait_ge(s_cin, 16 * 7)
            eng.wait_ge(s_const, NCONST)
            keys(0)
            turn_keys(0)
            gram(0)
            outs(0)
            squares(0)
            batches(eng, body)

            eng.wait_ge(s_oh, 1)
            eng.matmul(bank[0][:, 0:G * E], below[:, :], oh[:, :, 0, :], start=True, stop=False)
            for s in range(1, G):
                for k in range(TOPK):
                    eng.matmul(bank[0][:, s * E:G * E], ones16[:, :], oh[:, 0:G - s, k, :], start=False,
                               stop=False, skip_group_check=True)
            eng.matmul(bank[0][:, 0:G * E], below[:, :], oh[:, :, 1, :], start=False, stop=True)
            eng.matmul(bank[1][:, 0:G * TOPK * E], ones16[:, :], oh[:, :, :, :].rearrange("p g k e -> p (g k e)"),
                       start=True, stop=True).then_inc(s_cntp, 1)
            eng.wait_ge(s_ohr, 1)
            eng.wait_ge(s_rq, 1)
            for c in range(G * TOPK):
                mm = eng.matmul(bank[2][:, 0:NQ], oh_r[:, c, :], oh_q[:, c, :], start=(c == 0), stop=(c == G * TOPK - 1))
            mm.then_inc(s_tab, 1)

            W12N, W3N = DC * 2 * H, HC * D

            def turn_rows(j, r):
                if not exists(2 * j + r):
                    return
                t = 2 * j + r
                eng.wait_ge(s_ng[r], 16 * (j + 1))
                wait(eng, s_mT, t)
                for c in range(DC):
                    mm = eng.transpose(bank[5][:, c * P:(c + 1) * P], ng[r][:, c * P:(c + 1) * P], ident[:, :])
                mm.then_inc(s_mTp, 1)

            def up(e, half_, r):
                for c in range(DC):
                    mm = eng.matmul(bank[2 * half_ + r][:, 0:H], nTm[r][:, c * P:(c + 1) * P],
                                    W12[:, bass.ds(e * W12N + (2 * c + half_) * H, H)], start=(c == 0), stop=(c == DC - 1))
                return mm

            def tile(j, r):
                t = 2 * j + r
                if exists(t):
                    e = eng.value_load(ecoli[0:1, bass.ds(t, 1)], min_val=0, max_val=E - 1)
                    eng.wait_ge(s_mT, t + 1)
                    wait(eng, s_a, t - 1)
                    up(e, 0, r).then_inc(s_ap, 1)
                if exists(t - 1):
                    eng.wait_ge(s_h, t)
                    wait(eng, s_hT, 2 * (t - 1))
                    for c, (h0, n) in enumerate(HCH):
                        mm = eng.transpose(bank[6][0:n, c * P:(c + 1) * P], hid[1 - r][:, h0:h0 + n], ident[:, :])
                    mm.then_inc(s_hTp, 1)
                if exists(t):
                    wait(eng, s_h, t - 1)
                    up(e, 1, r).then_inc(s_bp, 1)
                turn_rows(j + (1 if r else 0), 1 - r)
                if exists(t - 1):
                    e = eng.value_load(ecoli[0:1, bass.ds(t - 1, 1)], min_val=0, max_val=E - 1)
                    eng.wait_ge(s_hT, 2 * t)
                    wait(eng, s_y, t - 2)
                    for c, (h0, n) in enumerate(HCH):
                        mm = eng.matmul(bank[4 if r else 7][:, :], hT[1 - r][0:n, c, :],
                                        W3[0:n, bass.ds(e * W3N + c * D, D)], start=(c == 0), stop=(c == HC - 1))
                    mm.then_inc(s_yp, 1)

            eng.wait_ge(s_et, 1)
            eng.wait_ge(s_wt, 16 * 3 * E)
            turn_rows(0, 0)
            expert_tiles(eng, tile)


def kernel(x, ctx_512, L0_xattn_W_k, L0_xattn_b_k, L0_xattn_ln_gamma, L0_xattn_ln_beta, L0_ffn_Wg, L0_ffn_W1, L0_ffn_W2, L0_ffn_W3):
    import concourse.bacc as bacc
    from concourse.bass_utils import run_bass_kernel_spmd

    def chunks(a):
        return np.ascontiguousarray(a.reshape(-1, P, a.shape[-1]).transpose(1, 0, 2))

    x = np.asarray(x)
    w1, w2, w3 = np.asarray(L0_ffn_W1), np.asarray(L0_ffn_W2), np.asarray(L0_ffn_W3)
    w12 = np.stack([w1.transpose(0, 2, 1), w2.transpose(0, 2, 1)], axis=2)
    w3t = w3.transpose(0, 2, 1)
    arrays = {
        "x": np.ascontiguousarray(x.reshape(T, D)),
        "xT": np.stack([chunks(x[b].T).reshape(P, DC * N) for b in range(B)]),
        "ctxT": np.ascontiguousarray(np.asarray(ctx_512).reshape(T, C).T),
        "wkT": np.ascontiguousarray(np.asarray(L0_xattn_W_k).T),
        "bk": np.asarray(L0_xattn_b_k).reshape(P, 1),
        "gamma": np.asarray(L0_xattn_ln_gamma).reshape(1, N),
        "beta": np.asarray(L0_xattn_ln_beta).reshape(1, N),
        "wgT": chunks(np.asarray(L0_ffn_Wg).T),
        "w12": np.stack([chunks(w12[e].reshape(D, 2 * H)).reshape(P, DC * 2 * H) for e in range(E)]),
        "w3a": np.stack([chunks(w3t[e][:2 * P]) for e in range(E)]),
        "w3b": np.ascontiguousarray(w3t[:, 2 * P:]),
    }
    nc = bacc.Bacc("TRN2", target_bir_lowering=False, num_devices=1)
    aps = [nc.dram_tensor(f"in_{k}", v.shape, F32, kind="ExternalInput").ap() for k, v in arrays.items()]
    out = nc.dram_tensor("out_0", [T + P, D], F32, kind="ExternalOutput").ap()
    build(nc, *aps, out)
    r = run_bass_kernel_spmd(nc, [{f"in_{k}": v for k, v in arrays.items()}], core_ids=[0])
    return r.results[0]["out_0"][:T].reshape(B, N, D)
```

```python
from contextlib import ExitStack

import numpy as np
import concourse.bass as bass
from concourse import mybir

ALU = mybir.AluOpType
ACT = mybir.ActivationFunctionType
F32, F16, BF16, I32, U32 = mybir.dt.float32, mybir.dt.float16, mybir.dt.bfloat16, mybir.dt.int32, mybir.dt.uint32
AX = mybir.AxisListType

P = 128
B, N, D = 4, 512, 512
C = 128
E, H = 8, 352
T = B * N
TPB = N // P
G = T // P
DC = D // P
HCH = [(0, 128), (128, 128), (256, 96)]
HC = len(HCH)
TOPK = 2
NT = (TOPK * T + E * (P - 1)) // P
NQ = NT + 1
ROW = D + 4
XEPS, SEPS = 1e-5, 1e-6
NTHR = T // P
W12N, W3N = DC * 2 * H, HC * D
WH = W12N // 2
AHEAD, AHEAD_LOW = 3, 1
WARM_GATHER = 28
NSCALE = 2.0 ** 10
WSCALE = 2.0 ** 15


def wait(eng, sem, value):
    if isinstance(value, int) and value <= 0:
        return
    eng.wait_ge(sem, value)


def build(nc, x, xT, ctxT, wkT, bk, gamma, beta, wgT, w12, w3a, w3b, out):
    ctx = ExitStack()
    with ctx:
        def sb(name, shape, dt=F32):
            return ctx.enter_context(nc.sbuf_tensor(name, shape, dt))

        def sem(name):
            return ctx.enter_context(nc.semaphore(name))

        bank = [ctx.enter_context(nc.psum_tensor(f"bank{i}", [P, 512], F32)) for i in range(8)]
        n_table = nc.dram_tensor("n_table", [T, ROW], F32, kind="Internal").ap()

        W12 = sb("W12", [P, E * W12N])
        stage = sb("stage", [P, 2 * W12N])
        parts = [[stage[:, r * W12N:(r + 1) * W12N].bitcast(F16)[:, k * W12N:(k + 1) * W12N] for k in range(2)] for r in range(2)]
        W3 = sb("W3", [P, E * W3N])
        xT_s = stage[:, 0:DC * N]
        ctx_s = stage[:, DC * N:DC * N + T]
        wjunk_a, wjunk_v = [stage[:, DC * N + T + k * WH // 2:DC * N + T + (k + 1) * WH // 2].bitcast(BF16) for k in range(2)]
        wk_s = sb("wk_s", [P, C])
        bk_s = sb("bk_s", [P, 1])
        wg_s = sb("wg_s", [P, DC, E])
        gam_s = sb("gam_s", [P, N])
        beta_s = sb("beta_s", [P, N])
        x_s = sb("x_s", [P, TPB, D])
        kv_s = sb("kv_s", [P, N])
        kvg_s = sb("kvg_s", [P, N])
        kvj_s = sb("kvj_s", [P, TPB, C])
        G_s = sb("G_s", [P, C])
        oT_s = sb("oT_s", [P, N])
        prod_s = sb("prod_s", [P, N])
        L_s = sb("L_s", [P, 2, N])
        x1_s = sb("x1_s", [P, 2, D])
        n_s = sb("n_s", [P, 2, D])
        nT_s = sb("nT_s", [P, 2, D])
        junk = sb("junk", [P, D])
        ident = sb("ident", [P, P])
        below = sb("below", [P, P], F16)
        ones16 = sb("ones16", [P, P], F16)
        iota = sb("iota", [P, P])
        thr = sb("thr", [P, NTHR])
        tok1 = sb("tok1", [P, G])
        dump1 = sb("dump1", [P, 1])
        half = sb("half", [P, 1])
        inv_d = sb("inv_d", [P, 1])
        eps_x = sb("eps_x", [P, 1])
        spare_v = sb("spare_v", [1, 16])
        spare_a = sb("spare_a", [P, 2])
        spare_p = sb("spare_p", [1, 16])
        ones = sb("ones", [P, P])
        guard = sb("guard", [P, 2])
        wsq = sb("wsq", [P, 4])
        wsum = sb("wsum", [P, 2])
        wrs = sb("wrs", [P, 2])
        wscale = sb("wscale", [P, E])
        wscalet = sb("wscalet", [P, NQ])
        wrec = sb("wrec", [P, 2])
        winv = sb("winv", [P, E])
        invt = sb("invt", [P, NQ])
        zero8 = sb("zero8", [P, E])
        ksum = sb("ksum", [P, 1])
        kneg = sb("kneg", [P, 1])
        msq = sb("msq", [P, TPB])
        bn = sb("bn", [P, 2, 6])
        mv = sb("mv", [P, 2, 2])
        va = sb("va", [P, 2])
        alpha = sb("alpha", [P, 2])
        lmin = sb("lmin", [P, 2])
        esum = sb("esum", [P, 2])
        einv = sb("einv", [P, 2])
        xsum = sb("xsum", [P, 2])
        xneg = sb("xneg", [P, 2])
        ssq = sb("ssq", [P, 2])
        vd = sb("vd", [P, 2])
        vr = sb("vr", [P, 2])
        rstd = sb("rstd", [P, 2])
        sc = sb("sc", [P, E])
        top = sb("top", [P, TPB, 8])
        topi = sb("topi", [P, TPB, 8], U32)
        dlt = sb("dlt", [P, G])
        edl = sb("edl", [P, G])
        wden = sb("wden", [P, G])
        wrow = sb("wrow", [P, G, 4])
        oh = sb("oh", [P, G, TOPK, E], F16)
        cnt = sb("cnt", [P, E])
        cmp_n = sb("cmp_n", [P, E, NTHR])
        ntile = sb("ntile", [P, E])
        tend = sb("tend", [P, E])
        start = sb("start", [P, E])
        base = sb("base", [P, G, E])
        pick = sb("pick", [P, G * TOPK, E])
        pos = sb("pos", [P, G * TOPK])
        posi = sb("posi", [P, G * TOPK], I32)
        qi = sb("qi", [P, G * TOPK], I32)
        ri = sb("ri", [P, G * TOPK], I32)
        qf = sb("qf", [P, G * TOPK])
        rf = sb("rf", [P, G * TOPK])
        tfree = sb("tfree", [P, 2 * NQ])
        gidx = sb("gidx", [P, NQ], U32)
        sidx = sb("sidx", [P, NQ], U32)
        gcol = sb("gcol", [P, 2], U32)
        scol = sb("scol", [P, 2], U32)
        ecol = sb("ecol", [P, NQ])
        ecoli = sb("ecoli", [P, NQ], I32)
        oh_r = xT_s[:, 0:G * TOPK * P // 2].bitcast(F16).rearrange("p (c r) -> p c r", r=P)
        oh_q = ctx_s[:, 0:G * TOPK * NQ // 2].bitcast(F16).rearrange("p (c q) -> p c q", q=NQ)
        cmp_t, cmp_u = [ctx_s[:, 1024 + k * NQ * E:1024 + (k + 1) * NQ * E].rearrange("p (t e) -> p t e", e=E) for k in range(2)]
        zrow = prod_s
        x_flat = x_s[:, :, :].rearrange("p a n -> p (a n)")
        ng = [x_flat[:, k * ROW:(k + 1) * ROW] for k in range(2)]
        nTm = [v[:, :].bitcast(F16) for v in (kvg_s, kv_s)]
        act_a = [L_s[:, k, 0:H] for k in range(2)]
        hid = [x1_s[:, k, 0:H] for k in range(2)]
        hT = [n_s[:, k, 0:HC * P].rearrange("p (c m) -> p c m", m=P) for k in range(2)]
        ym = [oT_s[:, :], kvj_s[:, :, :].rearrange("p a n -> p (a n)")]
        wm = sb("wm", [P, 2])
        wsel = sb("wsel", [P, 2])
        wmul = sb("wmul", [P, 2])

        s_const = sem("s_const")
        s_key = sem("s_key")
        s_gam = sem("s_gam")
        s_cin = sem("s_cin")
        s_zst = sem("s_zst")
        s_xT = sem("s_xT")
        s_xl = [sem(f"s_xl{i}") for i in range(TPB)]
        s_we, s_wo = sem("s_we"), sem("s_wo")
        s_w3 = sem("s_w3")
        s_wqa, s_wqv, s_wqp, s_wsum, s_wrs, s_wsc, s_winv = [
            sem(n) for n in ("s_wqa", "s_wqv", "s_wqp", "s_wsum", "s_wrs", "s_wsc", "s_winv")]
        s_wx = sem("s_wx")
        s_hi, s_lo = sem("s_hi"), sem("s_lo")
        s_stx = [sem(f"s_stx{i}") for i in range(2)]
        s_stn = [sem(f"s_stn{i}") for i in range(2)]
        s_wst = sem("s_wst")
        s_zr = sem("s_zr")
        s_ngam = sem("s_ngam")
        s_kvp, s_kv, s_kneg, s_kvc, s_kvjp, s_kvj = [sem(n) for n in ("s_kvp", "s_kv", "s_kneg", "s_kvc", "s_kvjp", "s_kvj")]
        s_Gp, s_G, s_op, s_o, s_ogp, s_prod, s_mp, s_msq, s_kvg = [
            sem(n) for n in ("s_Gp", "s_G", "s_op", "s_o", "s_ogp", "s_prod", "s_mp", "s_msq", "s_kvg")]
        s_dl, s_ed, s_wd, s_w1, s_w2, s_wi = [sem(n) for n in ("s_dl", "s_ed", "s_wd", "s_w1", "s_w2", "s_wi")]
        s_bn, s_mv, s_va, s_al, s_S, s_T, s_L, s_E, s_ei, s_x1 = [
            sem(n) for n in ("s_bn", "s_mv", "s_va", "s_al", "s_S", "s_T", "s_L", "s_E", "s_ei", "s_x1")]
        s_xn, s_sq, s_vd, s_vr, s_rs, s_n, s_nTp, s_nT, s_scp, s_sc, s_top, s_ti = [
            sem(n) for n in ("s_xn", "s_sq", "s_vd", "s_vr", "s_rs", "s_n", "s_nTp", "s_nT", "s_scp", "s_sc", "s_top", "s_ti")]
        s_r = sem("s_r")
        s_oh, s_cntp, s_ohq, s_rq, s_ohr, s_tab, s_et = [
            sem(n) for n in ("s_oh", "s_cntp", "s_ohq", "s_rq", "s_ohr", "s_tab", "s_et")]
        s_idx = sem("s_idx")
        s_ng = [sem(f"s_ng{i}") for i in range(2)]
        s_mTp, s_mT, s_ml, s_ap, s_a, s_bp, s_h, s_hTp, s_hT, s_yp, s_y, s_ws, s_wm = [
            sem(n) for n in ("s_mTp", "s_mT", "s_ml", "s_ap", "s_a", "s_bp", "s_h", "s_hTp", "s_hT", "s_yp", "s_y", "s_ws", "s_wm")]
        s_sct, s_gc, s_scc = sem("s_sct"), sem("s_gc"), sem("s_scc")

        NCONST = 15

        def hold(eng, site, *waits):
            for s, v in waits:
                wait(eng, s, v)
            if all(isinstance(v, int) for _, v in waits):
                return
            if eng is nc.vector or eng.engine == nc.vector.engine:
                eng.memset(spare_v[:, site:site + 1], 0.0)
            else:
                eng.tensor_tensor(spare_p[0:1, site:site + 1], half[0:1, :], half[0:1, :], ALU.add)

        def lag(b, i, k):
            while k > i:
                b, i = b - 1, i + TPB
            return b, i - k

        def lead(b, i, k=1):
            return (b, i + k) if i + k < TPB else (b + 1, i + k - TPB)

        def real(b):
            return not isinstance(b, int) or 0 <= b < B

        def body_slots(b):
            return [(b - 1, TPB - 1)] + [(b, i) for i in range(TPB - 1)]

        def batches(eng, slot, after=None, weights=None):
            def body(b):
                for q, (b_, i) in enumerate(body_slots(b)):
                    slot(b_, i)
                    if weights:
                        weights(b, q)
                if after:
                    after(b)
            body(0)
            with eng.Fori(1, B - 1) as b:
                body(b)
            body(B - 1)
            body(B)

        def g_of(b, i):
            return b * TPB + i

        FIRST, PAIRS = 3, (NT - 2 - 3) // 2

        def expert_tiles(eng, body):
            for t in range(FIRST):
                body(t // 2, t % 2)
            with eng.Fori(FIRST // 2, FIRST // 2 + PAIRS) as j:
                body(j, 1)
                body(j + 1, 0)
            for t in range(FIRST + 2 * PAIRS, NT + 1):
                body(t // 2, t % 2)

        def second(j, r):
            return isinstance(j, int) and (j, r) == (0, 1)

        def exists(t):
            return not isinstance(t, int) or 0 <= t < NT

        block = ctx.enter_context(nc.Block())

        @block.sync
        def _(eng):
            xrows = x.rearrange("(g p) d -> g p d", p=P)
            orows = out[0:T, :].rearrange("(g p) d -> g p d", p=P)
            nrows = n_table.rearrange("(g p) d -> g p d", p=P)
            for dst, src in ((wk_s[:, :], wkT), (ctx_s[:, 0:N], ctxT[:, 0:N]), (bk_s[:, :], bk)):
                eng.dma_start(dst, src).then_inc(s_key, 16)
            eng.dma_start(xT_s, xT[0]).then_inc(s_xT, 16)
            for dst, src in ((gam_s[:, :], gamma.to_broadcast([P, N])), (beta_s[:, :], beta.to_broadcast([P, N]))):
                eng.dma_start(dst, src).then_inc(s_gam, 16)
            for i in range(TPB):
                eng.dma_start(x_s[:, i, :], xrows[i]).then_inc(s_xl[i], 16)
            for dst, src in ((wg_s[:, :, :], wgT), (ctx_s[:, N:T], ctxT[:, N:T])):
                eng.dma_start(dst, src).then_inc(s_cin, 16)

            w3v = W3[:, :].rearrange("p (c d) -> p c d", d=D)

            def load_w12(e, s_w, before):
                wait(eng, s_w, 16 * before)
                eng.dma_start(W12[:, bass.ds(e * W12N, W12N)], w12[bass.ds(e, 1)].rearrange("a p n -> (a p) n")).then_inc(s_w, 16)

            def load_w3(e):
                wait(eng, s_w3, 32 * e)
                one = bass.ds(e, 1)
                eng.dma_start(w3v[:, bass.ds(e * HC, 2), :], w3a[one].rearrange("a p c d -> (a p) c d")).then_inc(s_w3, 16)
                eng.dma_start(w3v[0:HCH[2][1], bass.ds(e * HC + 2, 1), :].rearrange("p c d -> p (c d)"),
                              w3b[one].rearrange("a p d -> (a p) d")).then_inc(s_w3, 16)

            def weights(b, q):
                if q == 1 and real(b + 1):
                    load_w12(2 * b + 2, s_we, b + 1)
                if q == 2 and real(b):
                    load_w3(b)
                if q == 3 and real(b + 1):
                    load_w12(2 * b + 3, s_wo, b + 1)
            load_w12(0, s_we, 0)
            load_w12(1, s_wo, 0)

            def slot(b, i):
                if i == TPB - 1 and real(b + 2) and not (isinstance(b, int) and b < -1):
                    eng.wait_ge(s_op, b + 2)
                    eng.dma_start(xT_s, xT[bass.ds(b + 2, 1)].rearrange("a p n -> p (a n)")).then_inc(s_xT, 16)
                b1, i1 = lag(b, i, 1)
                if real(b1):
                    g = g_of(b1, i1)
                    eng.wait_ge(s_x1, g + 1)
                    eng.dma_start(orows[bass.ds(g, 1)].rearrange("a p d -> (a p) d"), x1_s[:, i1 % 2, :]).then_inc(s_stx[i1 % 2], 16)
                    if real(b1 + 1):
                        eng.dma_start(x_s[:, i1, :], xrows[bass.ds(g + TPB, 1)].rearrange("a p d -> (a p) d")).then_inc(s_xl[i1], 16)
                    eng.wait_ge(s_n, g + 1)
                    eng.dma_start(nrows[bass.ds(g, 1), :, 0:D].rearrange("a p d -> (a p) d"), n_s[:, i1 % 2, :]).then_inc(s_stn[i1 % 2], 16)

            def router_store(b):
                if isinstance(b, int) and b == 0:
                    return
                eng.wait_ge(s_w2, b)
                eng.wait_ge(s_wi, b)
                eng.dma_start(nrows[bass.ds((b - 1) * TPB, TPB), :, D:ROW].rearrange("g p k -> p g k"),
                              wrow[:, bass.ds((b - 1) * TPB, TPB), :]).then_inc(s_wst, 16)
            batches(eng, slot, router_store, weights)
            eng.wait_ge(s_zr, 1)
            eng.dma_start(out[T:T + P, :], zrow[:, :]).then_inc(s_zst, 16)
            for e in range(B, E):
                load_w3(e)
            eng.wait_ge(s_sct, 16 * NT)

        @block.gpsimd
        def _(eng):
            eng.memset(ident[:, :], 0.0).then_inc(s_const, 1)
            eng.memset(below[:, :], 1.0).then_inc(s_const, 1)
            eng.memset(ones[:, :], 1.0).then_inc(s_const, 1)
            eng.memset(half[:, :], -0.5).then_inc(s_const, 1)
            eng.memset(inv_d[:, :], 1.0 / D).then_inc(s_const, 1)
            eng.memset(eps_x[:, :], XEPS).then_inc(s_const, 1)
            eng.memset(guard[:, :], 1e-30).then_inc(s_const, 1)
            eng.wait_ge(s_const, 7)
            eng.affine_select(out=ident[:, :], in_=ident[:, :], compare_op=ALU.not_equal, fill=1.0, base=0,
                              pattern=[[-1, P]], channel_multiplier=1).then_inc(s_const, 1)
            eng.affine_select(out=below[:, :], in_=below[:, :], compare_op=ALU.is_gt, fill=0.0, base=0,
                              pattern=[[1, P]], channel_multiplier=-1).then_inc(s_const, 1)
            eng.memset(ones16[:, :], 1.0).then_inc(s_const, 1)
            eng.memset(zero8[:, :], 0.0).then_inc(s_const, 1)
            for dst, step, n, first, mul in ((iota, 1, P, 0, 0), (thr, P, NTHR, 0, 0), (tok1, P, G, 1, 1), (dump1, 0, 1, T + 1, 1)):
                eng.iota(dst[:, :], [[step, n]], base=first, channel_multiplier=mul,
                         allow_small_or_imprecise_dtypes=True).then_inc(s_const, 1)

            def scale(b, i):
                g, k = g_of(b, i), i % 2
                eng.wait_ge(s_va, g + 1)
                wait(eng, s_T, g - 1)
                eng.tensor_tensor(alpha[:, k:k + 1], va[:, k:k + 1], half[:, :], ALU.pow).then_inc(s_al, 1)

            def norm(b, i):
                g, k = g_of(b, i), i % 2
                eng.wait_ge(s_sq, g + 1)
                eng.tensor_tensor(vd[:, k:k + 1], ssq[:, k:k + 1], inv_d[:, :], ALU.mult).then_inc(s_vd, 1)
                eng.wait_ge(s_vd, g + 1)
                eng.tensor_tensor(vr[:, k:k + 1], vd[:, k:k + 1], eps_x[:, :], ALU.add).then_inc(s_vr, 1)
                eng.wait_ge(s_vr, g + 1)
                wait(eng, s_n, g - 1)
                eng.tensor_tensor(rstd[:, k:k + 1], vr[:, k:k + 1], half[:, :], ALU.pow).then_inc(s_rs, 1)
                hold(eng, 0, (s_rs, g + 1), (s_stn[k], 16 * (b * TPB // 2 + i // 2)), (s_nTp, g - 1))
                eng.tensor_scalar(n_s[:, k, :], x1_s[:, k, :], xneg[:, k:k + 1], rstd[:, k:k + 1], ALU.add, ALU.mult).then_inc(s_n, 1)

            def gamma_keys(b):
                eng.wait_ge(s_kvc, b + 1)
                wait(eng, s_ngam, 2 if isinstance(b, int) else 0)
                wait(eng, s_S, TPB * b)
                eng.tensor_tensor(kvg_s[:, :], kv_s[:, :], gam_s[:, :], ALU.mult).then_inc(s_kvg, 1)

            def slot(b, i):
                bn_, in_ = lead(b, i)
                if real(bn_):
                    scale(bn_, in_)
                if i == 2 and real(b):
                    eng.wait_ge(s_wsum, 2 * b + 2)
                    wait(eng, s_winv, 2 * b)
                    eng.tensor_tensor(wrs[:, :], wsum[:, :], half[:, 0:1].to_broadcast([P, 2]), ALU.pow).then_inc(s_wrs, 1)
                b1, i1 = lag(b, i, 1)
                if real(b1):
                    norm(b1, i1)
                if i == 1 and real(b + 1):
                    gamma_keys(b + 1)
            gamma_keys(0)
            batches(eng, slot)

            eng.wait_ge(s_mp, B)
            eng.memset(zrow[:, :], 0.0).then_inc(s_zr, 1)
            eng.wait_ge(s_ohq, 1)
            eng.wait_ge(s_const, NCONST)
            eng.tensor_tensor(oh_q.rearrange("p (g k) q -> p g (k q)", k=TOPK), oh_q.rearrange("p (g k) q -> p g (k q)", k=TOPK),
                              tok1[:, :, None].to_broadcast([P, G, TOPK * NQ]), ALU.mult).then_inc(s_rq, 1)

            eng.wait_ge(s_idx, 1)
            for i in range(2):
                eng.wait_ge(s_stx[i], 16 * G // 2)
                eng.wait_ge(s_stn[i], 16 * G // 2)
            eng.wait_ge(s_wst, 16 * B)
            eng.wait_ge(s_zst, 16)

            def gather(j, r):
                t = 2 * j + r
                if not exists(t):
                    return
                wait(eng, s_mTp, t - 1)
                wait(eng, s_ws, t - 1)
                wait(eng, s_wm, t - 1)
                eng.tensor_copy(gcol[:, r:r + 1], gidx[:, bass.ds(t, 1)]).then_inc(s_gc, 1)
                hold(eng, 1, (s_gc, t + 1))
                eng.indirect_dma_start(out=ng[r], out_offset=None, in_=n_table,
                                       in_offset=bass.IndirectOffsetOnAxis(ap=gcol[:, r:r + 1], axis=0)).then_inc(s_ng[r], 16)

            def body(j, r):
                gather(j + 1, r)
                t = 2 * j + r - 1
                if exists(t):
                    eng.tensor_copy(scol[:, 1 - r:2 - r], sidx[:, bass.ds(t, 1)]).then_inc(s_scc, 1)
                    hold(eng, 2, (s_scc, t + 1), (s_y, t + 1), (s_sct, 16 * t))
                    eng.indirect_dma_start(out=out, out_offset=bass.IndirectOffsetOnAxis(ap=scol[:, 1 - r:2 - r], axis=0),
                                           in_=ym[1 - r], in_offset=None, compute_op=ALU.add).then_inc(s_sct, 16)
            gather(0, 0)
            gather(0, 1)
            eng.wait_ge(s_idx, 2)
            expert_tiles(eng, body)

        @block.scalar
        def _(eng):
            eng.wait_ge(s_const, 4)
            eng.activation(spare_a[:, 0:1], half[:, :], ACT.Exp)

            def kv_evac(b):
                eng.wait_ge(s_kvp, b + 1)
                wait(eng, s_kvg, b)
                wait(eng, s_kneg, b)
                eng.activation(kv_s[:, :], bank[0][:, :], ACT.Identity, bias=bk_s[:, 0:1], accum_out=ksum[:, 0:1]).then_inc(s_kv, 1)

            def kvj_evac(b):
                eng.wait_ge(s_kvjp, b + 1)
                wait(eng, s_op, b)
                eng.activation(kvj_s[:, :, :].rearrange("p a n -> p (a n)"), bank[1][:, :], ACT.Copy).then_inc(s_kvj, 1)

            def o_evac(b):
                eng.wait_ge(s_op, b + 1)
                wait(eng, s_S, TPB * b)
                wait(eng, s_prod, b)
                eng.activation(oT_s[:, :], bank[1][:, :], ACT.Copy).then_inc(s_o, 1)

            def scaled(b, i):
                g, k = g_of(b, i), i % 2
                eng.wait_ge(s_S, g + 1)
                eng.wait_ge(s_al, g + 1)
                wait(eng, s_x1, g - 1)
                eng.activation(L_s[:, k, :], bank[2 + i][:, :], ACT.Copy, scale=alpha[:, k:k + 1]).then_inc(s_T, 1)

            def slot(b, i):
                b3, i3 = lag(b, i, 3)
                if real(b3):
                    g = g_of(b3, i3)
                    eng.wait_ge(s_nTp, g + 1)
                    eng.wait_ge(s_scp, g + 1)
                    eng.activation(nT_s[:, i3 % 2, :], bank[6][:, :], ACT.Copy).then_inc(s_nT, 1)
                if real(b):
                    g, k = g_of(b, i), i % 2
                    eng.wait_ge(s_L, g + 1)
                    wait(eng, s_ei, g - 1)
                    eng.activation(L_s[:, k, :], L_s[:, k, :], ACT.Exp, scale=-1.0, bias=lmin[:, k:k + 1],
                                   accum_out=esum[:, k:k + 1]).then_inc(s_E, 1)
                bn_, in_ = lead(b, i)
                if real(bn_):
                    scaled(bn_, in_)
                b1, i1 = lag(b, i, 1)
                if real(b1):
                    g, k = g_of(b1, i1), i1 % 2
                    eng.wait_ge(s_xn, g + 1)
                    wait(eng, s_vd, g - 1)
                    wait(eng, s_sq, g)
                    eng.activation(junk[:, :], x1_s[:, k, :], ACT.Square, bias=xneg[:, k:k + 1],
                                   accum_out=ssq[:, k:k + 1]).then_inc(s_sq, 1)
                if i == 2 and real(b + 1):
                    o_evac(b + 1)
                if i == 3 and real(b + 2):
                    kv_evac(b + 2)
                if i == 0 and real(b + 1):
                    kvj_evac(b + 1)
                if real(b3) and i3 == 3:
                    eng.wait_ge(s_dl, b3 + 1)
                    cols = bass.ds(b3 * TPB, TPB)
                    eng.activation(edl[:, cols], dlt[:, cols], ACT.Exp).then_inc(s_ed, 1)

            def weights(b, q):
                if q < 2 and real(b):
                    eng.wait_ge(s_we, 16 * (b + 1))
                    wait(eng, s_wqp, b)
                    wait(eng, s_wqa, 2 * b + q)
                    eng.activation(wjunk_a, W12[:, bass.ds(2 * b * W12N + q * WH, WH)], ACT.Square,
                                   accum_out=wsq[:, q:q + 1]).then_inc(s_wqa, 1)

            eng.wait_ge(s_key, 16 * 3)
            kv_evac(0)
            kvj_evac(0)
            o_evac(0)
            batches(eng, slot, None, weights)

            eng.activation(spare_a[:, 1:2], half[:, :], ACT.Silu)

            def mT_evac(j, r):
                t = 2 * j + r
                if exists(t):
                    eng.wait_ge(s_mTp, t + 1)
                    wait(eng, s_bp, t - 1)
                    eng.activation(nTm[r][:, 0:D], bank[5][:, :], ACT.Copy, scale=NSCALE).then_inc(s_mT, 1)

            def high_parts(j, r, chunks):
                t = 2 * j + r
                if not exists(t):
                    return
                e = eng.value_load(ecoli[0:1, bass.ds(t, 1)], min_val=0, max_val=E - 1)
                wait(eng, s_bp, t - 1)
                for c in chunks:
                    eng.activation(parts[r][0][:, c * 2 * H:(c + 1) * 2 * H], W12[:, bass.ds(e * W12N + c * 2 * H, 2 * H)], ACT.Copy,
                                   scale=wscalet[:, bass.ds(t, 1)]).then_inc(s_hi, 1)

            def tile(j, r):
                t = 2 * j + r
                j1, r1 = j + (1 if r else 0), 1 - r
                if exists(t):
                    eng.wait_ge(s_ap, t + 1)
                    wait(eng, s_h, t - 1)
                    eng.activation(act_a[r], bank[r][:, 0:H], ACT.Silu, scale=invt[:, bass.ds(t, 1)]).then_inc(s_a, 1)
                if exists(t - 1):
                    eng.wait_ge(s_hTp, t)
                    wait(eng, s_yp, t - 2)
                    for c, (_, n) in enumerate(HCH):
                        if c == 0:
                            eng.activation(hT[1 - r][:, 0:2, :].rearrange("p c m -> p (c m)"), bank[6][:, 0:2 * P], ACT.Copy).then_inc(s_hT, 1)
                        if c == 2:
                            eng.activation(hT[1 - r][0:n, 2, :], bank[6][0:n, 2 * P:3 * P], ACT.Copy).then_inc(s_hT, 1)
                high_parts(j1, r1, range(AHEAD, DC))
                if not second(j1, r1):
                    mT_evac(j1, r1)
                high_parts(j + 1, r, range(AHEAD))
                if exists(t - 1):
                    eng.wait_ge(s_yp, t)
                    eng.wait_ge(s_wm, t)
                    wait(eng, s_sct, 16 * (t - 2))
                    eng.activation(ym[1 - r], bank[4 if r else 7][:, :], ACT.Copy, scale=wm[:, 1 - r:2 - r]).then_inc(s_y, 1)
            eng.wait_ge(s_wx, 1)
            eng.wait_ge(s_et, 1)
            eng.wait_ge(s_tab, 1)
            eng.wait_ge(s_we, 16 * E // 2)
            eng.wait_ge(s_wo, 16 * E // 2)
            high_parts(0, 0, range(DC))
            mT_evac(0, 0)
            eng.wait_ge(s_wx, 2)
            high_parts(0, 1, range(AHEAD - 1))
            mT_evac(0, 1)
            high_parts(0, 1, range(AHEAD - 1, AHEAD))
            expert_tiles(eng, tile)

        @block.vector
        def _(eng):
            def centre_keys(b):
                eng.wait_ge(s_kv, b + 1)
                eng.tensor_scalar(kneg[:, :], ksum[:, :], -1.0 / N, None, ALU.mult).then_inc(s_kneg, 1)
                eng.wait_ge(s_kneg, b + 1)
                eng.tensor_scalar(kv_s[:, :], kv_s[:, :], kneg[:, 0:1], None, ALU.add).then_inc(s_kvc, 1)

            def gram_copy(b):
                eng.wait_ge(s_Gp, b + 1)
                wait(eng, s_ogp, b)
                eng.tensor_scalar(G_s[:, :], bank[0][:, 0:C], 1.0 / N, None, ALU.mult).then_inc(s_G, 1)

            def square_in(b):
                eng.wait_ge(s_ogp, b + 1)
                eng.wait_ge(s_o, b + 1)
                wait(eng, s_mp, b)
                eng.tensor_tensor(prod_s[:, :], bank[0][:, :], oT_s[:, :], ALU.mult).then_inc(s_prod, 1)

            def mean_square(b):
                eng.wait_ge(s_mp, b + 1)
                eng.tensor_scalar(msq[:, :], bank[1][:, 0:TPB], N * SEPS * XEPS, None, ALU.add).then_inc(s_msq, 1)

            def x_stats(b, i):
                g, k = g_of(b, i), i % 2
                eng.wait_ge(s_xl[i], 16 * (b + 1))
                eng.bn_stats(bn[:, k, :], x_s[:, i, :]).then_inc(s_bn, 1)
                hold(eng, 3, (s_bn, g + 1))
                eng.bn_aggr(mv[:, k, :], bn[:, k, :]).then_inc(s_mv, 1)

            def scale_in(b, i):
                g, k = g_of(b, i), i % 2
                eng.wait_ge(s_mv, g + 1)
                eng.wait_ge(s_msq, b + 1)
                wait(eng, s_al, g - 1)
                eng.tensor_scalar(va[:, k:k + 1], mv[:, k, 1:2], N * SEPS, msq[:, i:i + 1], ALU.mult, ALU.add).then_inc(s_va, 1)

            def router(b):
                cols = bass.ds(b * TPB, TPB)
                eng.wait_ge(s_ti, TPB * (b + 1) + 1)
                eng.tensor_tensor(dlt[:, cols], top[:, :, 1],
                                  top[:, :, 0], ALU.subtract).then_inc(s_dl, 1)
                eng.tensor_copy(wrow[:, cols, 2:4], topi[:, :, 0:2]).then_inc(s_wi, 1)

            def router_weights(b):
                cols = bass.ds(b * TPB, TPB)
                eng.wait_ge(s_ed, b + 1)
                eng.tensor_scalar(wden[:, cols], edl[:, cols], 1.0, None, ALU.add).then_inc(s_wd, 1)
                eng.wait_ge(s_wd, b + 1)
                w1 = wrow[:, cols, 0:1].rearrange("p g a -> p (g a)")
                w2 = wrow[:, cols, 1:2].rearrange("p g a -> p (g a)")
                eng.reciprocal(w1, wden[:, cols]).then_inc(s_w1, 1)
                eng.wait_ge(s_w1, b + 1)
                eng.tensor_tensor(w2, edl[:, cols], w1, ALU.mult).then_inc(s_w2, 1)

            def weight_sums(b):
                eng.wait_ge(s_wqp, b + 1)
                wait(eng, s_wrs, b)
                eng.tensor_reduce(wsum[:, :], bank[7][:, E:E + 4].rearrange("p (k h) -> p k h", h=2), AX.X, ALU.add).then_inc(s_wsum, 1)
                eng.wait_ge(s_wsum, 2 * b + 1)
                eng.tensor_tensor(wsum[:, :], wsum[:, :], guard[:, :], ALU.max).then_inc(s_wsum, 1)

            def weight_scale(b):
                eng.wait_ge(s_wrs, b + 1)
                eng.tensor_scalar(wscale[:, bass.ds(2 * b, 2)], wrs[:, :], WSCALE, None, ALU.mult).then_inc(s_wsc, 1)
                eng.reciprocal(wrec[:, :], wrs[:, :]).then_inc(s_winv, 1)
                eng.wait_ge(s_winv, 2 * b + 1)
                eng.tensor_scalar(winv[:, bass.ds(2 * b, 2)], wrec[:, :], 1.0 / (WSCALE * NSCALE), None, ALU.mult).then_inc(s_winv, 1)

            def weights(b, q):
                if q < 2 and real(b):
                    eng.wait_ge(s_wo, 16 * (b + 1))
                    wait(eng, s_wqp, b)
                    first = isinstance(b, int) and b == 0
                    for h in ([[], [0, 1]][q] if first else [q]):
                        half_w = W12[:, bass.ds((2 * b + 1) * W12N + h * WH, WH)]
                        wait(eng, s_wqv, 2 * b + h)
                        eng.scalar_tensor_tensor(wjunk_v, half_w, 1.0, half_w, ALU.mult, ALU.mult,
                                                 accum_out=wsq[:, 2 + h:3 + h]).then_inc(s_wqv, 1)
                if q == 3 and real(b):
                    weight_scale(b)

            def slot(b, i):
                if i == 3 and real(b + 1):
                    square_in(b + 1)
                bn_, in_ = lead(b, i)
                if real(bn_):
                    x_stats(bn_, in_)
                    if i < TPB - 1:
                        scale_in(bn_, in_)
                if real(b):
                    g, k = g_of(b, i), i % 2
                    hold(eng, 4, (s_T, g + 1), (s_E, g - 1))
                    eng.tensor_tensor_reduce(L_s[:, k, :], L_s[:, k, :], beta_s[:, :], 1.0, 3.0e38, ALU.add, ALU.min,
                                             lmin[:, k:k + 1]).then_inc(s_L, 1)
                b1, i1 = lag(b, i, 1)
                if real(b1):
                    g, k = g_of(b1, i1), i1 % 2
                    eng.wait_ge(s_E, g + 1)
                    eng.reciprocal(einv[:, k:k + 1], esum[:, k:k + 1]).then_inc(s_ei, 1)
                    eng.wait_ge(s_ei, g + 1)
                    wait(eng, s_stx[k], 16 * (b1 * TPB // 2 + i1 // 2))
                    wait(eng, s_sq, g - 1)
                    wait(eng, s_n, g - 1)
                    eng.scalar_tensor_tensor(x1_s[:, k, :], L_s[:, k, :], einv[:, k:k + 1], x_s[:, i1, :], ALU.mult, ALU.add,
                                             accum_out=xsum[:, k:k + 1]).then_inc(s_x1, 1)
                    eng.wait_ge(s_x1, g + 1)
                    eng.tensor_scalar(xneg[:, k:k + 1], xsum[:, k:k + 1], -1.0 / D, None, ALU.mult).then_inc(s_xn, 1)
                if i == TPB - 1 and real(bn_):
                    mean_square(bn_)
                    scale_in(bn_, in_)
                if i == 2 and real(b + 1):
                    gram_copy(b + 1)
                weights(*((b + 1, 0) if i == TPB - 1 else (b, i + 1)))
                if i == 3 and real(b + 2):
                    centre_keys(b + 2)
                b3, i3 = lag(b, i, 3)
                if real(b3):
                    g = g_of(b3, i3)
                    eng.wait_ge(s_scp, g + 3)
                    eng.wait_ge(s_ti, g + 1)
                    eng.tensor_copy(sc[:, :], bank[7][:, 0:E]).then_inc(s_sc, 1)
                    hold(eng, 5, (s_sc, g + 2))
                    eng.max(top[:, i3, :], sc[:, :]).then_inc(s_top, 1)
                    hold(eng, 6, (s_top, g + 1))
                    eng.max_index(topi[:, i3, :], top[:, i3, :], sc[:, :]).then_inc(s_ti, 1)
                    if i3 == 3:
                        router(b3)
                        if not isinstance(b, int) or b < B:
                            router_weights(b3)
                if i == 1 and real(b):
                    weight_sums(b)
            eng.memset(spare_v[:, 12:13], 0.0).then_inc(s_scp, 1)
            eng.memset(spare_v[:, 13:14], 0.0).then_inc(s_scp, 1)
            eng.memset(spare_v[:, 14:15], 0.0).then_inc(s_sc, 1)
            eng.memset(spare_v[:, 15:16], 0.0).then_inc(s_ti, 1)
            centre_keys(0)
            eng.wait_ge(s_gam, 16 * 2)
            eng.tensor_scalar(gam_s[:, :], gam_s[:, :], -1.0, None, ALU.mult).then_inc(s_ngam, 1)
            eng.tensor_scalar(beta_s[:, :], beta_s[:, :], -1.0, None, ALU.mult).then_inc(s_ngam, 1)
            gram_copy(0)

            batches(eng, slot)

            steps = [0]

            def then(ins):
                steps[0] += 1
                ins.then_inc(s_r, 1)
                eng.wait_ge(s_r, steps[0])

            eng.wait_ge(s_const, NCONST)
            eng.wait_ge(s_wi, B)
            eng.wait_ge(s_op, B)
            eng.tensor_tensor(oh[:, :, :, :], wrow[:, :, 2:4, None].to_broadcast([P, G, TOPK, E]),
                              iota[:, None, None, 0:E].to_broadcast([P, G, TOPK, E]), ALU.is_equal).then_inc(s_oh, 1)
            router_weights(B - 1)
            eng.wait_ge(s_cntp, 1)
            then(eng.tensor_reduce(cnt[:, :], bank[1][:, 0:G * TOPK * E].rearrange("p (c e) -> p e c", e=E), AX.X, ALU.add))
            then(eng.tensor_tensor(cmp_n[:, :, :], cnt[:, :, None].to_broadcast([P, E, NTHR]),
                                   thr[:, None, :].to_broadcast([P, E, NTHR]), ALU.is_gt))
            then(eng.tensor_reduce(ntile[:, :], cmp_n[:, :, :], AX.X, ALU.add))
            then(eng.tensor_tensor_scan(tend[:, :], ntile[:, :], zero8[:, :], 0.0, ALU.add, ALU.add))
            then(eng.tensor_tensor(start[:, :], tend[:, :], ntile[:, :], ALU.subtract))
            then(eng.tensor_scalar(start[:, :], start[:, :], float(P), None, ALU.mult))
            then(eng.tensor_tensor(base[:, :, :], bank[0][:, 0:G * E].rearrange("p (g e) -> p g e", e=E),
                                   start[:, None, :].to_broadcast([P, G, E]), ALU.add))
            then(eng.tensor_tensor(pick[:, :, :].rearrange("p (g k) e -> p g k e", k=TOPK), oh[:, :, :, :],
                                   base[:, :, None, :].to_broadcast([P, G, TOPK, E]), ALU.mult))
            then(eng.tensor_reduce(pos[:, :], pick[:, :, :], AX.X, ALU.add))
            then(eng.tensor_copy(posi[:, :], pos[:, :]))
            eng.tensor_scalar(ri[:, :], posi[:, :], P - 1, None, ALU.bitwise_and).then_inc(s_r, 1)
            eng.tensor_scalar(qi[:, :], posi[:, :], 7, None, ALU.arith_shift_right).then_inc(s_r, 1)
            steps[0] += 2
            eng.wait_ge(s_r, steps[0])
            eng.tensor_copy(qf[:, :], qi[:, :]).then_inc(s_r, 1)
            steps[0] += 1
            then(eng.tensor_copy(rf[:, :], ri[:, :]))
            eng.tensor_tensor(oh_q, qf[:, :, None].to_broadcast([P, G * TOPK, NQ]),
                              iota[:, None, 0:NQ].to_broadcast([P, G * TOPK, NQ]), ALU.is_equal).then_inc(s_ohq, 1)
            for h in range(2):
                cols = slice(h * G * TOPK // 2, (h + 1) * G * TOPK // 2)
                eng.tensor_tensor(oh_r[:, cols, :], rf[:, cols, None].to_broadcast([P, G * TOPK // 2, P]),
                                  iota[:, None, :].to_broadcast([P, G * TOPK // 2, P]), ALU.is_equal).then_inc(s_ohr, 1)
            then(eng.tensor_tensor(cmp_t, iota[:, 0:NQ, None].to_broadcast([P, NQ, E]),
                                   tend[:, None, :].to_broadcast([P, NQ, E]), ALU.is_ge))
            then(eng.tensor_reduce(ecol[:, :], cmp_t, AX.X, ALU.add))
            then(eng.tensor_scalar(ecol[:, :], ecol[:, :], float(E - 1), None, ALU.min))
            eng.tensor_copy(ecoli[:, :], ecol[:, :]).then_inc(s_et, 1)
            eng.wait_ge(s_tab, 1)
            eng.tensor_scalar(gidx[:, :], bank[2][:, 0:NQ], -1.0, 0.0, ALU.add, ALU.max).then_inc(s_idx, 1)
            eng.wait_ge(s_wsc, B)
            eng.wait_ge(s_winv, 2 * B)
            then(eng.tensor_tensor(cmp_t, ecol[:, :, None].to_broadcast([P, NQ, E]),
                                   iota[:, None, 0:E].to_broadcast([P, NQ, E]), ALU.is_equal))
            then(eng.tensor_tensor(cmp_u, cmp_t, wscale[:, None, :].to_broadcast([P, NQ, E]), ALU.mult))
            eng.tensor_reduce(wscalet[:, :], cmp_u, AX.X, ALU.add).then_inc(s_wx, 1)
            then(eng.tensor_tensor(cmp_t, cmp_t, winv[:, None, :].to_broadcast([P, NQ, E]), ALU.mult))
            eng.tensor_reduce(invt[:, :], cmp_t, AX.X, ALU.add).then_inc(s_wx, 1)
            then(eng.tensor_scalar(tfree[:, 0:NQ], bank[2][:, 0:NQ], 0.0, dump1[:, 0:1], ALU.is_equal, ALU.mult))
            eng.scalar_tensor_tensor(sidx[:, :], bank[2][:, 0:NQ], -1.0, tfree[:, 0:NQ], ALU.add, ALU.add).then_inc(s_idx, 1)

            def low_parts(j, r, chunks):
                t = 2 * j + r
                if not exists(t):
                    return
                e = eng.value_load(ecoli[0:1, bass.ds(t, 1)], min_val=0, max_val=E - 1)
                for c in chunks:
                    cols = slice(c * 2 * H, (c + 1) * 2 * H)
                    eng.wait_ge(s_hi, DC * t + c + 1)
                    eng.scalar_tensor_tensor(parts[r][1][:, cols], W12[:, bass.ds(e * W12N + c * 2 * H, 2 * H)],
                                             wscalet[:, bass.ds(t, 1)], parts[r][0][:, cols], ALU.mult, ALU.subtract).then_inc(s_lo, 1)

            def low_rows(j, r):
                t = 2 * j + r
                if not exists(t):
                    return
                eng.wait_ge(s_mT, t + 1)
                eng.scalar_tensor_tensor(nTm[r][:, D:2 * D], bank[5][:, :], NSCALE, nTm[r][:, 0:D], ALU.mult,
                                         ALU.subtract).then_inc(s_ml, 1)

            def tile(j, r):
                t = 2 * j + r
                if not exists(t):
                    return
                eng.wait_ge(s_ng[r], 16 * (j + 1))
                wait(eng, s_wm, t)
                eng.tensor_scalar(wsel[:, :], ng[r][:, D + 2:D + 4], ecol[:, bass.ds(t, 1)], None, ALU.is_equal).then_inc(s_ws, 1)
                hold(eng, 7, (s_ws, t + 1), (s_y, t - 1))
                eng.tensor_tensor_reduce(wmul[:, :], wsel[:, :], ng[r][:, D:D + 2], 1.0, 0.0, ALU.mult, ALU.add,
                                         wm[:, r:r + 1]).then_inc(s_wm, 1)
                low_parts(j + (1 if r else 0), 1 - r, range(AHEAD_LOW, DC))
                eng.wait_ge(s_a, t + 1)
                eng.wait_ge(s_bp, t + 1)
                wait(eng, s_hTp, t - 1)
                eng.scalar_tensor_tensor(hid[r], bank[2 + r][:, 0:H], invt[:, bass.ds(t, 1)], act_a[r], ALU.mult, ALU.mult).then_inc(s_h, 1)
                if not second(j + (1 if r else 0), 1 - r):
                    low_rows(j + (1 if r else 0), 1 - r)
                low_parts(j + 1, r, range(AHEAD_LOW))
            eng.wait_ge(s_wx, 2)
            eng.wait_ge(s_et, 1)
            low_parts(0, 0, range(DC - 1))
            low_rows(0, 0)
            low_parts(0, 0, range(DC - 1, DC))
            low_parts(0, 1, range(AHEAD_LOW))
            low_rows(0, 1)
            expert_tiles(eng, tile)

        @block.tensor
        def _(eng):
            def warm(moving, times):
                for _ in range(times):
                    eng.matmul(bank[7][:, 0:moving.shape[-1]], ones16[:, :], moving, start=True, stop=True)

            def keys(b):
                wait(eng, s_prod, b)
                eng.matmul(bank[0][:, :], wk_s[:, :], ctx_s[:, bass.ds(b * N, N)], start=True, stop=True).then_inc(s_kvp, 1)

            def turn_keys(b):
                eng.wait_ge(s_kvc, b + 1)
                wait(eng, s_msq, b)
                for c in range(TPB):
                    mm = eng.transpose(bank[1][:, c * C:(c + 1) * C], kv_s[:, c * P:(c + 1) * P], ident[:, :])
                mm.then_inc(s_kvjp, 1)

            def gram(b):
                eng.wait_ge(s_kvj, b + 1)
                eng.wait_ge(s_kv, b + 1)
                for c in range(TPB):
                    mm = eng.matmul(bank[0][:, 0:C], kvj_s[:, c, :], kvj_s[:, c, :], start=(c == 0), stop=(c == TPB - 1))
                mm.then_inc(s_Gp, 1)

            def outs(b):
                eng.wait_ge(s_xT, 16 * (b + 1))
                eng.wait_ge(s_kvj, b + 1)
                for c in range(DC):
                    mm = eng.matmul(bank[1][:, :], kvj_s[:, c, :], xT_s[:, c * N:(c + 1) * N], start=(c == 0), stop=(c == DC - 1))
                mm.then_inc(s_op, 1)

            def gram_outs(b):
                eng.wait_ge(s_G, b + 1)
                eng.wait_ge(s_o, b + 1)
                eng.matmul(bank[0][:, :], G_s[:, :], oT_s[:, :], start=True, stop=True).then_inc(s_ogp, 1)

            def squares(b):
                eng.wait_ge(s_prod, b + 1)
                for i in range(TPB):
                    mm = eng.matmul(bank[1][:, i:i + 1], prod_s[:, i * P:(i + 1) * P], ones[:, 0:1], start=True, stop=True)
                mm.then_inc(s_mp, 1)

            def sims(b, i):
                g = g_of(b, i)
                eng.wait_ge(s_o, b + 1)
                eng.wait_ge(s_kvg, b + 1)
                wait(eng, s_T, g - TPB + 1)
                eng.matmul(bank[2 + i][:, :], oT_s[:, i * P:(i + 1) * P], kvg_s[:, :], start=True, stop=True).then_inc(s_S, 1)

            def turn_n(b, i):
                if real(b):
                    g, k = g_of(b, i), i % 2
                    eng.wait_ge(s_n, g + 1)
                    wait(eng, s_nT, g)
                    for c in range(DC):
                        mm = eng.transpose(bank[6][:, c * P:(c + 1) * P], n_s[:, k, c * P:(c + 1) * P], ident[:, :])
                    mm.then_inc(s_nTp, 1)

            def weight_norms(b):
                if not isinstance(b, int) or b > 0:
                    eng.wait_ge(s_sc, g_of(*lag(b, 1, 3)) + 1)
                eng.wait_ge(s_wqa, 2 * b + 2)
                eng.wait_ge(s_wqv, 2 * b + 2)
                eng.matmul(bank[7][:, E:E + 4], ones[:, :], wsq[:, :], start=True, stop=True).then_inc(s_wqp, 1)

            def slot(b, i):
                draining = isinstance(b, int) and b >= B
                if draining:
                    turn_n(*lag(b, i, 2))
                if i == 3 and real(b + 1):
                    squares(b + 1)
                if i == 1 and real(b + 1):
                    gram(b + 1)
                if i == 1 and real(b):
                    weight_norms(b)
                if i == 2 and real(b):
                    eng.wait_ge(s_wsum, 2 * b + 1)
                b3, i3 = lag(b, i, 3)
                if real(b3):
                    g = g_of(b3, i3)
                    eng.wait_ge(s_nT, g + 1)
                    eng.wait_ge(s_sc, g + 1)
                    for c in range(DC):
                        mm = eng.matmul(bank[7][:, 0:E], nT_s[:, i3 % 2, c * P:(c + 1) * P], wg_s[:, c, :], start=(c == 0), stop=(c == DC - 1))
                    mm.then_inc(s_scp, 1)
                ba, ia = lead(b, i, 2)
                if real(ba) and i != 2:
                    sims(ba, ia)
                if not draining:
                    turn_n(*lag(b, i, 2))
                if i == 1 and real(b + 1):
                    outs(b + 1)
                if i == 2 and real(b + 1):
                    gram_outs(b + 1)
                    sims(ba, ia)
                if i == 3 and real(b + 2):
                    keys(b + 2)
                if i == 0 and real(b + 1):
                    turn_keys(b + 1)

            eng.wait_ge(s_const, NCONST)
            eng.wait_ge(s_key, 16 * 3)
            keys(0)
            turn_keys(0)
            gram(0)
            outs(0)
            gram_outs(0)
            sims(0, 0)
            eng.wait_ge(s_cin, 16 * 2)

            batches(eng, slot)

            eng.wait_ge(s_oh, 1)
            eng.matmul(bank[0][:, 0:G * E], below[:, :], oh[:, :, 0, :], start=True, stop=False)
            for s in range(1, G):
                for k in range(TOPK):
                    eng.matmul(bank[0][:, s * E:G * E], ones16[:, :], oh[:, 0:G - s, k, :], start=False,
                               stop=False, skip_group_check=True)
            eng.matmul(bank[0][:, 0:G * E], below[:, :], oh[:, :, 1, :], start=False, stop=True)
            eng.matmul(bank[1][:, 0:G * TOPK * E], ones16[:, :], oh[:, :, :, :].rearrange("p g k e -> p (g k e)"),
                       start=True, stop=True).then_inc(s_cntp, 1)
            eng.wait_ge(s_rq, 1)
            for c in range(G * TOPK):
                if c % G == 0:
                    eng.wait_ge(s_ohr, c // G + 1)
                mm = eng.matmul(bank[2][:, 0:NQ], oh_r[:, c, :], oh_q[:, c, :], start=(c == 0), stop=(c == G * TOPK - 1))
            mm.then_inc(s_tab, 1)
            warm(oh[:, :, :, :].rearrange("p g k e -> p (g k e)"), WARM_GATHER)

            def turn_rows(j, r):
                if not exists(2 * j + r):
                    return
                t = 2 * j + r
                eng.wait_ge(s_ng[r], 16 * (j + 1))
                wait(eng, s_mT, t)
                wait(eng, s_ml, t)
                for c in range(DC):
                    mm = eng.transpose(bank[5][:, c * P:(c + 1) * P], ng[r][:, c * P:(c + 1) * P], ident[:, :])
                mm.then_inc(s_mTp, 1)

            def up(t, which, r):
                for c in range(DC):
                    n_high, n_low = [nTm[r][:, k * D + c * P:k * D + (c + 1) * P] for k in range(2)]
                    w_high, w_low = [parts[r][k][:, (2 * c + which) * H:(2 * c + which + 1) * H] for k in range(2)]
                    if which == 0:
                        eng.wait_ge(s_lo, DC * t + c + 1)
                    for k, (n_, w_) in enumerate(((n_high, w_high), (n_high, w_low), (n_low, w_high))):
                        mm = eng.matmul(bank[2 * which + r][:, 0:H], n_, w_, start=(c == 0 and k == 0),
                                        stop=(c == DC - 1 and k == 2))
                return mm

            def tile(j, r):
                t = 2 * j + r
                if exists(t):
                    eng.wait_ge(s_ml, t + 1)
                    wait(eng, s_a, t - 1)
                    up(t, 0, r).then_inc(s_ap, 1)
                if exists(t - 1):
                    eng.wait_ge(s_h, t)
                    wait(eng, s_hT, 2 * (t - 1))
                    for c, (h0, n) in enumerate(HCH):
                        mm = eng.transpose(bank[6][0:n, c * P:(c + 1) * P], hid[1 - r][:, h0:h0 + n], ident[:, :])
                    mm.then_inc(s_hTp, 1)
                if exists(t):
                    wait(eng, s_h, t - 1)
                    up(t, 1, r).then_inc(s_bp, 1)
                if not second(j + (1 if r else 0), 1 - r):
                    turn_rows(j + (1 if r else 0), 1 - r)
                if exists(t - 1):
                    e = eng.value_load(ecoli[0:1, bass.ds(t - 1, 1)], min_val=0, max_val=E - 1)
                    eng.wait_ge(s_w3, 32 * e + 32)
                    eng.wait_ge(s_hT, 2 * t)
                    wait(eng, s_y, t - 2)
                    for c, (h0, n) in enumerate(HCH):
                        mm = eng.matmul(bank[4 if r else 7][:, :], hT[1 - r][0:n, c, :],
                                        W3[0:n, bass.ds(e * W3N + c * D, D)], start=(c == 0), stop=(c == HC - 1))
                    mm.then_inc(s_yp, 1)

            eng.wait_ge(s_et, 1)
            turn_rows(0, 0)
            turn_rows(0, 1)
            expert_tiles(eng, tile)


def kernel(x, ctx_512, L0_xattn_W_k, L0_xattn_b_k, L0_xattn_ln_gamma, L0_xattn_ln_beta, L0_ffn_Wg, L0_ffn_W1, L0_ffn_W2, L0_ffn_W3):
    import concourse.bacc as bacc
    from concourse.bass_utils import run_bass_kernel_spmd

    def chunks(a):
        return np.ascontiguousarray(a.reshape(-1, P, a.shape[-1]).transpose(1, 0, 2))

    x = np.asarray(x)
    w1, w2, w3 = np.asarray(L0_ffn_W1), np.asarray(L0_ffn_W2), np.asarray(L0_ffn_W3)
    w12 = np.stack([w1.transpose(0, 2, 1), w2.transpose(0, 2, 1)], axis=2)
    w3t = w3.transpose(0, 2, 1)
    arrays = {
        "x": np.ascontiguousarray(x.reshape(T, D)),
        "xT": np.stack([chunks(x[b].T).reshape(P, DC * N) for b in range(B)]),
        "ctxT": np.ascontiguousarray(np.asarray(ctx_512).reshape(T, C).T),
        "wkT": np.ascontiguousarray(np.asarray(L0_xattn_W_k).T),
        "bk": np.asarray(L0_xattn_b_k).reshape(P, 1),
        "gamma": np.asarray(L0_xattn_ln_gamma).reshape(1, N),
        "beta": np.asarray(L0_xattn_ln_beta).reshape(1, N),
        "wgT": chunks(np.asarray(L0_ffn_Wg).T),
        "w12": np.stack([chunks(w12[e].reshape(D, 2 * H)).reshape(P, DC * 2 * H) for e in range(E)]),
        "w3a": np.stack([chunks(w3t[e][:2 * P]) for e in range(E)]),
        "w3b": np.ascontiguousarray(w3t[:, 2 * P:]),
    }
    nc = bacc.Bacc("TRN2", target_bir_lowering=False, num_devices=1)
    aps = [nc.dram_tensor(f"in_{k}", v.shape, F32, kind="ExternalInput").ap() for k, v in arrays.items()]
    out = nc.dram_tensor("out_0", [T + P, D], F32, kind="ExternalOutput").ap()
    build(nc, *aps, out)
    r = run_bass_kernel_spmd(nc, [{f"in_{k}": v for k, v in arrays.items()}], core_ids=[0])
    return r.results[0]["out_0"][:T].reshape(B, N, D)
```
